# Optimizing a Trainium2 kernel written in Bass

```python
import numpy as np
import jax
import jax.numpy as jnp

def _softmax(x, axis=-1):
    return jax.nn.softmax(x, axis=axis)
def _gelu(x):
    return jax.nn.gelu(x, approximate=True)
def _silu(x):
    return jax.nn.silu(x)
def _sigmoid(x):
    return jax.nn.sigmoid(x)
def _layernorm(x, axis=-1, eps=1e-5):
    m = jnp.mean(x, axis=axis, keepdims=True)
    v = jnp.var(x, axis=axis, keepdims=True)
    return (x - m) / jnp.sqrt(v + eps)
def _scatter_add(tgt, idx, src, axis=0):
    return tgt.at[idx].add(src)
def _segment_sum(src, seg, n):
    return jax.ops.segment_sum(src, seg, n)

kernel_name = 'mk_lm_tower_d1_tok_ids512_8183c3'

def setup_inputs(seed: int = 0):
    np.random.seed(seed)
    _w = jnp.asarray
    def _rec_inputs():
        import jax
        import jax.numpy as jnp
        _rk = jax.random.key(seed)
        x = jax.random.randint(jax.random.fold_in(_rk, 1), (8, 1024), 0, 50256, jnp.int32)
        return x
    x = _rec_inputs()
    def _L0_tok_setup():
        import jax, jax.numpy as jnp
        import numpy as np
        NUM_EMBEDDINGS = 50257
        EMBED_SIZE = 512
        key = jax.random.key(seed)
        k1, k2 = jax.random.split(key)
        x = jax.random.randint(k1, (8, 2048), 0, NUM_EMBEDDINGS)
        embed_matrix = jax.random.normal(k2, (NUM_EMBEDDINGS, EMBED_SIZE), dtype=jnp.float32)
        return {'x': x, 'embed_matrix': embed_matrix}
    _L0_tok_all = _L0_tok_setup()
    _L0_tok_in = {k: v for k, v in _L0_tok_all.items() if k in ('embed_matrix', )}
    del _L0_tok_all

    def _L0_attn_setup():
        import jax, jax.numpy as jnp
        import numpy as np
        D = 512
        M = 64
        SE = 32
        SS = 64
        H = 4
        B, L = (2, 1024)
        BOT = max(D // 4, 32)

        def _layernorm(x, g, b, eps=1e-05):
            mu = jnp.mean(x, axis=-1, keepdims=True)
            var = jnp.var(x, axis=-1, keepdims=True)
            return (x - mu) * jax.lax.rsqrt(var + eps) * g + b

        def _forward(x, Wq, Wk, Wv, Wf, bf, Wo, ln_g, ln_b, eslots, Eq, Ek, Ev, Eo, know, Sin, Sg_w, Sg_b, So, C1w, C1b, C2w, C2b):
            b, l, d = x.shape
            scale = M ** (-0.5)
            q = (jax.nn.elu(x @ Wq) + 1.0) * scale
            k = jax.nn.elu(x @ Wk) + 1.0
            v = x @ Wv
            forget = jax.nn.sigmoid(x @ Wf + bf)
            log_f_cum = jnp.clip(jnp.cumsum(jnp.log(jnp.clip(forget, 1e-06, None)), axis=1), -20.0, 20.0)
            exp_neg = jnp.exp(-log_f_cum)
            exp_pos = jnp.exp(log_f_cum)
            kv = k[..., :, None] * v[..., None, :]
            cum_kv = jnp.cumsum(exp_neg[..., None] * kv, axis=1)
            Mstate = exp_pos[..., None] * cum_kv
            z = exp_pos * jnp.cumsum(exp_neg * k, axis=1)
            num = jnp.einsum('blm,blmd->bld', q, Mstate)
            den = jnp.einsum('blm,blm->bl', q, z)[..., None] + 1e-06
            w_out = _layernorm(num / den, ln_g, ln_b) @ Wo
            hd = D // H
            mem = jnp.broadcast_to(eslots, (b, SE, D))
            qh = (x @ Eq).reshape(b, l, H, hd)
            kh = (mem @ Ek).reshape(b, SE, H, hd)
            vh = (mem @ Ev).reshape(b, SE, H, hd)
            scores = jnp.einsum('blhe,bshe->bhls', qh, kh) / jnp.sqrt(jnp.float32(hd))
            attn = jax.nn.softmax(scores, axis=-1)
            e_out = jnp.einsum('bhls,bshe->blhe', attn, vh).reshape(b, l, D) @ Eo
            kb = jnp.broadcast_to(know, (b, SS, D))
            qs = x @ Sin
            s_scores = jnp.einsum('bld,bsd->bls', qs, kb) / jnp.sqrt(jnp.float32(D))
            s_attn = jax.nn.softmax(s_scores, axis=-1)
            retrieved = jnp.einsum('bls,bsd->bld', s_attn, kb)
            gate = jax.nn.sigmoid(x @ Sg_w + Sg_b)
            s_out = (gate * retrieved + (1.0 - gate) * x) @ So
            wts = jax.nn.softmax(jax.nn.silu(x @ C1w + C1b) @ C2w + C2b, axis=-1)
            fused = wts[..., 0:1] * w_out + wts[..., 1:2] * e_out + wts[..., 2:3] * s_out
            return fused
        key = jax.random.key(seed)
        ks = jax.random.split(key, 24)
        r = lambda i, shape, s=0.02: jax.random.normal(ks[i], shape, dtype=jnp.float32) * s
        return {'x': jax.random.normal(ks[0], (B, L, D), dtype=jnp.float32), 'Wq': r(1, (D, M)), 'Wk': r(2, (D, M)), 'Wv': r(3, (D, D)), 'Wf': r(4, (D, M)), 'bf': jnp.zeros((M,), jnp.float32), 'Wo': r(5, (D, D)), 'ln_g': jnp.ones((D,), jnp.float32), 'ln_b': jnp.zeros((D,), jnp.float32), 'eslots': r(6, (1, SE, D)), 'Eq': r(7, (D, D)), 'Ek': r(8, (D, D)), 'Ev': r(9, (D, D)), 'Eo': r(10, (D, D)), 'know': r(11, (1, SS, D)), 'Sin': r(12, (D, D)), 'Sg_w': r(13, (D, D)), 'Sg_b': jnp.zeros((D,), jnp.float32), 'So': r(14, (D, D)), 'C1w': r(15, (D, BOT)), 'C1b': jnp.zeros((BOT,), jnp.float32), 'C2w': r(16, (BOT, 3)), 'C2b': jnp.zeros((3,), jnp.float32)}
    _L0_attn_all = _L0_attn_setup()
    _L0_attn_in = {k: v for k, v in _L0_attn_all.items() if k in ('Wq', 'Wk', 'Wv', 'Wf', 'bf', 'Wo', 'ln_g', 'ln_b', 'eslots', 'Eq', 'Ek', 'Ev', 'Eo', 'know', 'Sin', 'Sg_w', 'Sg_b', 'So', 'C1w', 'C1b', 'C2w', 'C2b', )}
    del _L0_attn_all

    def _L0_ffn_setup():
        import jax, jax.numpy as jnp
        import numpy as np
        B, S, H, E, K, DF, SH = (8, 4096, 512, 8, 2, 128, 512)
        key = jax.random.key(seed)
        ks = jax.random.split(key, 10)
        n = lambda i, shape, sc: jax.random.normal(ks[i], shape, jnp.float32) * sc
        return {'hidden_states': n(0, (B, S, H), 1.0), 'gate_w': n(1, (E, H), 0.05), 'w1': n(2, (E, H, DF), 0.05), 'b1': n(3, (E, DF), 0.01), 'w2': n(4, (E, DF, H), 0.05), 'b2': n(5, (E, H), 0.01), 'sw1': n(6, (H, SH), 0.05), 'sb1': n(7, (SH,), 0.01), 'sw2': n(8, (SH, H), 0.05), 'sb2': n(9, (H,), 0.01)}
    _L0_ffn_all = _L0_ffn_setup()
    _L0_ffn_in = {k: v for k, v in _L0_ffn_all.items() if k in ('gate_w', 'w1', 'b1', 'w2', 'b2', 'sw1', 'sb1', 'sw2', 'sb2', )}
    del _L0_ffn_all

    return {
        "x": x,
        "L0_tok_embed_matrix": _L0_tok_in["embed_matrix"],
        "L0_attn_Wq": _L0_attn_in["Wq"],
        "L0_attn_Wk": _L0_attn_in["Wk"],
        "L0_attn_Wv": _L0_attn_in["Wv"],
        "L0_attn_Wf": _L0_attn_in["Wf"],
        "L0_attn_bf": _L0_attn_in["bf"],
        "L0_attn_Wo": _L0_attn_in["Wo"],
        "L0_attn_ln_g": _L0_attn_in["ln_g"],
        "L0_attn_ln_b": _L0_attn_in["ln_b"],
        "L0_attn_eslots": _L0_attn_in["eslots"],
        "L0_attn_Eq": _L0_attn_in["Eq"],
        "L0_attn_Ek": _L0_attn_in["Ek"],
        "L0_attn_Ev": _L0_attn_in["Ev"],
        "L0_attn_Eo": _L0_attn_in["Eo"],
        "L0_attn_know": _L0_attn_in["know"],
        "L0_attn_Sin": _L0_attn_in["Sin"],
        "L0_attn_Sg_w": _L0_attn_in["Sg_w"],
        "L0_attn_Sg_b": _L0_attn_in["Sg_b"],
        "L0_attn_So": _L0_attn_in["So"],
        "L0_attn_C1w": _L0_attn_in["C1w"],
        "L0_attn_C1b": _L0_attn_in["C1b"],
        "L0_attn_C2w": _L0_attn_in["C2w"],
        "L0_attn_C2b": _L0_attn_in["C2b"],
        "L0_ffn_gate_w": _L0_ffn_in["gate_w"],
        "L0_ffn_w1": _L0_ffn_in["w1"],
        "L0_ffn_b1": _L0_ffn_in["b1"],
        "L0_ffn_w2": _L0_ffn_in["w2"],
        "L0_ffn_b2": _L0_ffn_in["b2"],
        "L0_ffn_sw1": _L0_ffn_in["sw1"],
        "L0_ffn_sb1": _L0_ffn_in["sb1"],
        "L0_ffn_sw2": _L0_ffn_in["sw2"],
        "L0_ffn_sb2": _L0_ffn_in["sb2"],
    }

def reference(x, L0_tok_embed_matrix, L0_attn_Wq, L0_attn_Wk, L0_attn_Wv, L0_attn_Wf, L0_attn_bf, L0_attn_Wo, L0_attn_ln_g, L0_attn_ln_b, L0_attn_eslots, L0_attn_Eq, L0_attn_Ek, L0_attn_Ev, L0_attn_Eo, L0_attn_know, L0_attn_Sin, L0_attn_Sg_w, L0_attn_Sg_b, L0_attn_So, L0_attn_C1w, L0_attn_C1b, L0_attn_C2w, L0_attn_C2b, L0_ffn_gate_w, L0_ffn_w1, L0_ffn_b1, L0_ffn_w2, L0_ffn_b2, L0_ffn_sw1, L0_ffn_sb1, L0_ffn_sw2, L0_ffn_sb2):
    import jax
    import jax.numpy as jnp
    def _L0_tok_ref(x, embed_matrix):
        import jax, jax.numpy as jnp
        import numpy as np
        NUM_EMBEDDINGS = 50257
        EMBED_SIZE = 512
        return jnp.take(embed_matrix, x, axis=0)

    def _L0_attn_ref(x, Wq, Wk, Wv, Wf, bf, Wo, ln_g, ln_b, eslots, Eq, Ek, Ev, Eo, know, Sin, Sg_w, Sg_b, So, C1w, C1b, C2w, C2b):
        import jax, jax.numpy as jnp
        import numpy as np
        D = 512
        M = 64
        SE = 32
        SS = 64
        H = 4
        B, L = (2, 1024)
        BOT = max(D // 4, 32)

        def _layernorm(x, g, b, eps=1e-05):
            mu = jnp.mean(x, axis=-1, keepdims=True)
            var = jnp.var(x, axis=-1, keepdims=True)
            return (x - mu) * jax.lax.rsqrt(var + eps) * g + b

        def _forward(x, Wq, Wk, Wv, Wf, bf, Wo, ln_g, ln_b, eslots, Eq, Ek, Ev, Eo, know, Sin, Sg_w, Sg_b, So, C1w, C1b, C2w, C2b):
            b, l, d = x.shape
            scale = M ** (-0.5)
            q = (jax.nn.elu(x @ Wq) + 1.0) * scale
            k = jax.nn.elu(x @ Wk) + 1.0
            v = x @ Wv
            forget = jax.nn.sigmoid(x @ Wf + bf)
            log_f_cum = jnp.clip(jnp.cumsum(jnp.log(jnp.clip(forget, 1e-06, None)), axis=1), -20.0, 20.0)
            exp_neg = jnp.exp(-log_f_cum)
            exp_pos = jnp.exp(log_f_cum)
            kv = k[..., :, None] * v[..., None, :]
            cum_kv = jnp.cumsum(exp_neg[..., None] * kv, axis=1)
            Mstate = exp_pos[..., None] * cum_kv
            z = exp_pos * jnp.cumsum(exp_neg * k, axis=1)
            num = jnp.einsum('blm,blmd->bld', q, Mstate)
            den = jnp.einsum('blm,blm->bl', q, z)[..., None] + 1e-06
            w_out = _layernorm(num / den, ln_g, ln_b) @ Wo
            hd = D // H
            mem = jnp.broadcast_to(eslots, (b, SE, D))
            qh = (x @ Eq).reshape(b, l, H, hd)
            kh = (mem @ Ek).reshape(b, SE, H, hd)
            vh = (mem @ Ev).reshape(b, SE, H, hd)
            scores = jnp.einsum('blhe,bshe->bhls', qh, kh) / jnp.sqrt(jnp.float32(hd))
            attn = jax.nn.softmax(scores, axis=-1)
            e_out = jnp.einsum('bhls,bshe->blhe', attn, vh).reshape(b, l, D) @ Eo
            kb = jnp.broadcast_to(know, (b, SS, D))
            qs = x @ Sin
            s_scores = jnp.einsum('bld,bsd->bls', qs, kb) / jnp.sqrt(jnp.float32(D))
            s_attn = jax.nn.softmax(s_scores, axis=-1)
            retrieved = jnp.einsum('bls,bsd->bld', s_attn, kb)
            gate = jax.nn.sigmoid(x @ Sg_w + Sg_b)
            s_out = (gate * retrieved + (1.0 - gate) * x) @ So
            wts = jax.nn.softmax(jax.nn.silu(x @ C1w + C1b) @ C2w + C2b, axis=-1)
            fused = wts[..., 0:1] * w_out + wts[..., 1:2] * e_out + wts[..., 2:3] * s_out
            return fused
        return _forward(x, Wq, Wk, Wv, Wf, bf, Wo, ln_g, ln_b, eslots, Eq, Ek, Ev, Eo, know, Sin, Sg_w, Sg_b, So, C1w, C1b, C2w, C2b)

    def _L0_ffn_ref(hidden_states, gate_w, w1, b1, w2, b2, sw1, sb1, sw2, sb2):
        import jax, jax.numpy as jnp
        import numpy as np
        B, S, H, E, K, DF, SH = (8, 4096, 512, 8, 2, 128, 512)
        x = hidden_states
        xf = x.reshape(-1, x.shape[-1])
        T = xf.shape[0]
        scores = jax.nn.softmax(xf @ gate_w.T, axis=-1)
        topk_w, topk_i = jax.lax.top_k(scores, K)
        topk_w = topk_w / (topk_w.sum(-1, keepdims=True) + 1e-20)
        combine = jnp.zeros((T, E), xf.dtype).at[jnp.arange(T)[:, None], topk_i].add(topk_w)
        h1 = jax.nn.relu(jnp.einsum('th,ehf->tef', xf, w1) + b1)
        eo = jnp.einsum('tef,efh->teh', h1, w2) + b2
        y = jnp.einsum('te,teh->th', combine, eo)
        shared = jax.nn.relu(xf @ sw1 + sb1) @ sw2 + sb2
        return (y + shared).reshape(x.shape)

    h = _L0_tok_ref(x, L0_tok_embed_matrix)
    h = h + _L0_attn_ref(_layernorm(h, axis=-1), L0_attn_Wq, L0_attn_Wk, L0_attn_Wv, L0_attn_Wf, L0_attn_bf, L0_attn_Wo, L0_attn_ln_g, L0_attn_ln_b, L0_attn_eslots, L0_attn_Eq, L0_attn_Ek, L0_attn_Ev, L0_attn_Eo, L0_attn_know, L0_attn_Sin, L0_attn_Sg_w, L0_attn_Sg_b, L0_attn_So, L0_attn_C1w, L0_attn_C1b, L0_attn_C2w, L0_attn_C2b)
    h = h + _L0_ffn_ref(_layernorm(h, axis=-1), L0_ffn_gate_w, L0_ffn_w1, L0_ffn_b1, L0_ffn_w2, L0_ffn_b2, L0_ffn_sw1, L0_ffn_sb1, L0_ffn_sw2, L0_ffn_sb2)
    return h


_drawn_inputs = setup_inputs


def setup_inputs(seed=0):
    import zlib

    import numpy as np

    out = dict(_drawn_inputs(seed))
    spreads = {'L0_attn_bf': (0.0, 2.0),
     'L0_attn_ln_g': (1.0, 0.2),
     'L0_attn_ln_b': (0.0, 0.351),
     'L0_attn_Sg_b': (0.0, 1.854),
     'L0_attn_C1b': (0.0, 0.8),
     'L0_attn_C2b': (0.0, 0.1)}
    factors = {'L0_attn_Wq': 5.711,
     'L0_attn_Wk': 3.09,
     'L0_attn_Wf': 58.459,
     'L0_attn_eslots': 8.0,
     'L0_attn_Eq': 8.0,
     'L0_attn_Ek': 8.0,
     'L0_attn_Ev': 8.0,
     'L0_attn_Eo': 8.0,
     'L0_attn_know': 64.0,
     'L0_attn_Sin': 64.0,
     'L0_attn_C1w': 3.578,
     'L0_attn_C2w': 3.383,
     'L0_ffn_b1': 30.467,
     'L0_ffn_b2': 8.0,
     'L0_ffn_sb1': 8.0,
     'L0_ffn_sb2': 8.0,
     'L0_attn_Sg_w': 3.039}
    for name, (base, spread) in spreads.items():
        noise = np.random.default_rng([zlib.crc32(name.encode()), seed]).standard_normal(out[name].shape)
        drawn = base * np.exp(spread * noise) if base else spread * noise
        out[name] = jnp.asarray(drawn.astype(out[name].dtype))
    for name, factor in factors.items():
        out[name] = (out[name] * factor).astype(out[name].dtype)
    return out
```

```python
from contextlib import ExitStack

import concourse.bass as bass
from concourse import mybir

F32 = mybir.dt.float32
F32R = mybir.dt.float32r
I32 = mybir.dt.int32
ALU = mybir.AluOpType
ACT = mybir.ActivationFunctionType
AX = mybir.AxisListType

P = 128
T = 4
GT = T * P
LN_EPS = 1e-5
DEN_EPS = 1e-6
FORGET_MIN = 1e-6
LOG_CLIP = 20.0
F_CLIP = -30.0
TOPK_EPS = 1e-20


def lm_tower(nc, x_idx, emb, Wq, Wk, Wv, Wf, bf, Wo, ln_g, ln_b, eslots, Eq, Ek, Ev, Eo, know, Sin, Sg_w, Sg_b,
             So, C1w, C1b, C2w, C2b, gate_w, w1, b1, w2, b2, sw1, sb1, sw2, sb2, out):
    NSEQ, _, TILES = x_idx.shape
    D = emb.shape[1]
    KB = D // P
    M = Wq.shape[1]
    SE, SS = eslots.shape[1], know.shape[1]
    HD = P
    H = D // HD
    BOT = C1w.shape[1]
    NE, _, DF = w1.shape
    GPS = TILES // T
    assert GPS == 2 and M == 64 and H * SE == P and BOT == P and DF == P and D == GT
    WES = H * SE + SS
    Q_SCALE = float(M) ** -0.5

    h_mid = nc.dram_tensor("h_mid", (NSEQ * GPS, T, P, D), F32, kind="Internal").ap()
    out_g = out.rearrange("b (u t p) d -> (b u) t p d", t=T, p=P)

    def blocks(w):
        return w.rearrange("(k p) n -> p k n", p=P)

    def split3(pe, o, wh, wl, mh, ml, start, stop):
        pe.matmul(o, wh, mh, start=start, stop=False)
        pe.matmul(o, wh, ml, start=False, stop=False)
        return pe.matmul(o, wl, mh, start=False, stop=stop)

    with ExitStack() as whole:
        bank = [whole.enter_context(nc.psum_tensor(f"bank{b}", [P, GT], F32)) for b in range(8)]
        ident = whole.enter_context(nc.sbuf_tensor("ident", [P, P], F32))
        half = whole.enter_context(nc.sbuf_tensor("half", [P, T], F32))
        pass_a(nc, locals())
        pass_b(nc, locals())



def pass_a(nc, e):
    (bank, ident, half, blocks, split3) = (e[n] for n in ("bank", "ident", "half", "blocks", "split3"))
    (NSEQ, TILES, D, KB, M, SE, SS, H, GPS, WES, Q_SCALE) = (
        e[n] for n in ("NSEQ", "TILES", "D", "KB", "M", "SE", "SS", "H", "GPS", "WES", "Q_SCALE"))
    x_idx, emb, h_mid = e["x_idx"], e["emb"], e["h_mid"]
    HS = H * SE

    with nc.cleanup_on_exit(), ExitStack() as ctx:
        def sb(name, shape, dt=F32):
            return ctx.enter_context(nc.sbuf_tensor(name, shape, dt))

        wqkf_h, wqkf_l = sb("wqkf_h", [P, KB, 4 * M], F32R), sb("wqkf_l", [P, KB, 4 * M], F32R)
        wc1_h, wc1_l = sb("wc1_h", [P, KB, P], F32R), sb("wc1_l", [P, KB, P], F32R)
        wes_h, wes_l = sb("wes_h", [P, KB, WES], F32R), sb("wes_l", [P, KB, WES], F32R)
        wv_h, wv_l = sb("wv_h", [P, KB, D], F32R), sb("wv_l", [P, KB, D], F32R)
        wsg_h, wsg_l = sb("wsg_h", [P, KB, D], F32R), sb("wsg_l", [P, KB, D], F32R)
        wso_h, wso_l = sb("wso_h", [P, KB, D], F32R), sb("wso_l", [P, KB, D], F32R)
        wwo_h, wwo_l = sb("wwo_h", [P, KB, D], F32R), sb("wwo_l", [P, KB, D], F32R)
        wve_h, wve_l = sb("wve_h", [P, D], F32R), sb("wve_l", [P, D], F32R)
        know_hl = sb("know_hl", [P, D], F32R)
        bias_wo = sb("bias_wo", [P, D])
        c2w = sb("c2w", [P, 3])
        c2b = sb("c2b", [P, 3])
        c1b = sb("c1b", [P, 1])
        sgb = sb("sgb", [P, KB])
        bff = sb("bff", [P, 1])
        sign = sb("sign", [P, 1])
        ones = sb("ones", [P, 1])
        causal = sb("causal", [P, P])

        prep_a(nc, e, locals())

        h = [sb(f"h{u}", [P, T, D]) for u in range(2)]
        idx = sb("idx", [P, TILES], I32)
        xn = sb("xn", [P, T, D])
        xT_h, xT_l = sb("xT_h", [P, KB, GT], F32R), sb("xT_l", [P, KB, GT], F32R)
        ef = sb("ef", [P, GT])
        dec = sb("dec", [P, GT])
        qk = sb("qk", [P, GT])
        mix1 = sb("mix1", [P, GT])
        am = sb("am", [P, GT])
        c1s = sb("c1s", [P, GT])
        gate_b, mix_b, xf_b = [ef, dec], [qk, mix1], [am, c1s]
        lraw = sb("lraw", [P, GT])
        carry = sb("carry", [P, 2])
        q2 = sb("q2", [P, GT])
        q2_h, q2_l = sb("q2_h", [P, GT], F32R), sb("q2_l", [P, GT], F32R)
        kf = sb("kf", [M, GT])
        kh = sb("kh", [M, GT], F32R)
        zc = sb("zc", [M, GT])
        k_hl = sb("k_hl", [P, GT], F32R)
        kT_hl = sb("kT_hl", [P, T, P], F32R)
        a_h, a_l = sb("a_h", [P, GT], F32R), sb("a_l", [P, GT], F32R)
        aT_h, aT_l = a_h, a_l
        sT_h, sT_l = q2_h, q2_l
        v_h, v_l = sb("v_h", [P, 2, D], F32R), sb("v_l", [P, 2, D], F32R)
        nT_h, nT_l = v_h, v_l
        s_h, s_l = sb("s_h", [P, D], F32R), sb("s_l", [P, D], F32R)
        n = sb("n", [P, 2, D])
        mixT_h, mixT_l = sb("mixT_h", [P, KB, GT], F32R), sb("mixT_l", [P, KB, GT], F32R)
        sx = sb("sx", [P, T, WES])
        pr = sb("pr", [P, T, 2 * P])
        mE, mS = sb("mE", [P, T, H]), sb("mS", [P, T])
        rs = sb("rs", [P, T, H + 1])
        bn6, mv, var_e = sb("bn6", [P, T, 6]), sb("mv", [P, T, 2]), sb("var_e", [P, T])
        rstd, nmr = sb("rstd", [P, T]), sb("nmr", [P, T])
        nb6, nmv, nv = sb("nb6", [P, T, 6]), sb("nmv", [P, T, 2]), sb("nv", [P, T])
        nrs, nsc, nbi = sb("nrs", [P, T]), sb("nsc", [P, T]), sb("nbi", [P, T])
        lg, lm, lsum = sb("lg", [P, T, 3]), sb("lm", [P, T]), sb("lsum", [P, T])
        w = sb("w", [P, T, 3])
        den, den2, rdw = sb("den", [P, T]), sb("den2", [P, T]), sb("rdw", [P, T])

        BY_PE = dict(xT_ps=T, c1_ps=1, f_ps=1, qk_ps=1, es_ps=2, v_ps=T, kT_ps=1, a_ps=1, small_ps=1,
                     state_ps=T, num_ps=T, nT_ps=T, aT_ps=1, sT_ps=1, ret_ps=KB, gate_ps=KB, so_ps=T, out_ps=T)
        BY_ACT = dict(xT_hi=T, c1_sig=1, f_exp=1, qk_exp=1, ln_u=1, decay=1, es_exp=2, q_hi=1, k_hi=2,
                      v_hi=T, w_exp=1, kT_sb=1, a_hi=1, s_hi=T, n_rows=T, nT_hi=T, aT_hi=1, sT_hi=1, gate=KB,
                      mix_hi=KB)
        BY_DVE = dict(ln_bn=T, ln_stats=T, ln_bias=1, xT_lo=T, silu=1, f_clip=1, qk_min=1, u=1, qk_elu=1, lsum_raw=1, l_clip=1, l_carry=1, q_dup=2,
                      k_dec=1, z_sum=1, z_carry=1, qz=1, q_lo=1, k_lo=1, es_max=4, es_sub=4, es_sum=2, es_rec=1, lg_add=1,
                      den_add=1, den_rec=1, den_sq=1, lg_max=1, lg_sub=1, w_sum=1, w_rec=1, w_done=1, rE_w=1, rd_w=1,
                      v_lo=T, a_mask=1, a_lo=1, s_lo=T, n_bn=T, n_stats=T, n_var=T, n_scale=T, n_bias=T, nT_lo=T, aT_lo=1,
                      sT_lo=1, xg=KB, mix_mul=KB, mix=KB, mix_lo=KB, h_bias=T, h_so=T, h_out=T)
        BY_POOL = dict(ln_var=1, ln_rstd=1, xn_rows=T, n_rstd=T, probs=3, xf=KB)
        BY_DMA = {**{f"h_in{t}": 1 for t in range(T)}, **{f"h_stored{t}": 1 for t in range(T)}}
        per = {**BY_PE, **BY_ACT, **BY_DVE, **BY_POOL, **BY_DMA}
        sem = {name: nc.alloc_semaphore("A_" + name) for name in per}
        idx_in = nc.alloc_semaphore("A_idx_in")

        def at(name, g, k=0):
            step = 16 if name in BY_DMA else 1
            before = g if name.startswith("h_in") else g + 1
            return before * (per[name] * step) + (k + 1) * step

        def wait(eng, name, g, k=0):
            eng.wait_ge(sem[name], at(name, g, k))

        unread = nc.alloc_semaphore("A_unread")

        def waits_end(eng):
            eng.sem_inc(unread, 1)

        def credit(eng, names, step=1):
            for name in names:
                eng.sem_inc(sem[name], per[name] * step)

        USES = [("c1", "silu", 0), ("f", "f_clip", 0), ("qk", "qk_elu", 0), ("es0", "es_sub", 1), ("es1", "es_sub", 3),
                ("v0", "v_lo", 0), ("v1", "v_lo", 1), ("kT", "kT_sb", 0), ("a", "a_mask", 0), ("small", "den_add", 0),
                ("gate0", "gate", 0), ("num0", "n_rows", 0), ("v2", "v_lo", 2), ("num1", "n_rows", 1),
                ("v3", "v_lo", 3), ("num2", "n_rows", 2), ("nT0", "nT_lo", 0), ("gate1", "gate", 1), ("nT1", "nT_lo", 1),
                ("num3", "n_rows", 3), ("sT", "sT_lo", 0), ("aT", "aT_lo", 0), ("gate2", "gate", 2),
                ("ret0", "mix_mul", 0), ("ret1", "mix_mul", 1), ("gate3", "gate", 3), ("ret2", "mix_mul", 2),
                ("ret3", "mix_mul", 3), ("out0", "h_out", 0), ("nT2", "nT_lo", 2), ("out1", "h_out", 1),
                ("nT3", "nT_lo", 3)]
        USES += [(f"so{t}", "h_so", t) for t in range(T)]
        USES += [(f"xT{t}", "xT_lo", t) for t in range(T)] + [("out2", "h_out", 2), ("out3", "h_out", 3)]
        RING = 7
        assert len(USES) % RING == 0
        place = {use[0]: i for i, use in enumerate(USES)}
        state = bank[RING]

        def ps(use):
            return bank[place[use] % RING]

        def bank_free(pe, use, g):
            i = place[use] - RING
            before, signal, k = USES[i]
            slot = g - 1 if i < 0 else g
            wait(pe, signal, slot + 1 if before.startswith("xT") else slot, k)

        def flat(t):
            return t.rearrange("p a b -> p (a b)")

        block = ctx.enter_context(nc.Block())

        def loop(eng, body):
            with eng.Fori(0, NSEQ - 1) as i:
                for u in range(GPS):
                    body(i * GPS + u, u, i, False)
            for u in range(GPS):
                body((NSEQ - 1) * GPS + u, u, NSEQ - 1, u == GPS - 1)

        @block.sync
        def _(sp):
            credit(sp, [f"h_stored{t}" for t in range(T)], 16)
            sp.dma_start(idx[:, :], x_idx[0]).then_inc(idx_in, 16)

            def body(g, u, i, last):
                if u == 0 and not (isinstance(i, int) and i == NSEQ - 1):
                    for t in range(T):
                        wait(sp, f"h_in{t}", g + 1)
                    sp.dma_start(idx[:, :], x_idx[i + 1]).then_inc(idx_in, 16)
                for t in range(T):
                    wait(sp, "h_so", g, t)
                    wait(sp, "h_out", g, t)
                    sp.dma_start(h_mid[g, t], h[u][:, t, :]).then_inc(sem[f"h_stored{t}"], 16)
            loop(sp, body)
            for t in range(T):
                wait(sp, f"h_stored{t}", NSEQ * GPS - 1)

        @block.gpsimd
        def _(pool):
            credit(pool, BY_POOL)

            def gather(g, u):
                for t in range(T):
                    if not (isinstance(g, int) and g < GPS):
                        wait(pool, f"h_stored{t}", g - 2)
                        waits_end(pool)
                    pool.indirect_dma_start(
                        out=h[u][:, t, :], out_offset=None, in_=emb[:, :],
                        in_offset=bass.IndirectOffsetOnAxis(ap=idx[:, u * T + t:u * T + t + 1], axis=0),
                    ).then_inc(sem[f"h_in{t}"], 16)

            def ln_scale(g):
                wait(pool, "ln_stats", g, T - 1)
                wait(pool, "ln_rstd", g - 1)
                waits_end(pool)
                pool.tensor_scalar(var_e[:, :], mv[:, :, 1], LN_EPS, None, ALU.add).then_inc(sem["ln_var"], 1)
                wait(pool, "ln_var", g)
                wait(pool, "xn_rows", g - 1, T - 1)
                pool.tensor_tensor(rstd[:, :], var_e[:, :], half[:, :], ALU.pow).then_inc(sem["ln_rstd"], 1)

            def ln_rows(g, u, tiles):
                wait(pool, "ln_bias", g)
                for t in tiles:
                    wait(pool, "xT_ps", g - 1, t)
                    waits_end(pool)
                    pool.tensor_scalar(xn[:, t, :], h[u][:, t, :], rstd[:, t:t + 1], nmr[:, t:t + 1],
                                       ALU.mult, ALU.add).then_inc(sem["xn_rows"], 1)

            pool.wait_ge(idx_in, 16)
            gather(0, 0)
            ln_scale(0)
            ln_rows(0, 0, range(T))

            def body(g, u, i, last):
                if not last:
                    if u == GPS - 1:
                        pool.wait_ge(idx_in, (i + 2) * 16)
                        waits_end(pool)
                    gather(g + 1, (u + 1) % GPS)
                wait(pool, "a_lo", g)
                wait(pool, "small_ps", g)
                xf(g, 0)
                xf(g, 1)
                for t in range(T):
                    wait(pool, "n_var", g, t)
                    pool.tensor_tensor(nrs[:, t:t + 1], nv[:, t:t + 1], half[:, 0:1], ALU.pow).then_inc(sem["n_rstd"], 1)
                    if t == 0:
                        wait(pool, "rE_w", g)
                        wait(pool, "es_exp", g, 1)
                        wait(pool, "aT_ps", g - 1)
                        pool.tensor_tensor(
                            pr[:, :, 0:HS].rearrange("p t (h s) -> p t h s", h=H),
                            sx[:, :, 0:HS].rearrange("p t (h s) -> p t h s", h=H),
                            rs[:, :, 0:H].unsqueeze(3).to_broadcast([P, T, H, SE]), ALU.mult).then_inc(sem["probs"], 1)
                        for z in range(2):
                            pool.tensor_tensor(
                                pr[:, :, HS + z * SS:HS + (z + 1) * SS], sx[:, :, HS:WES],
                                rs[:, :, H:H + 1].to_broadcast([P, T, SS]), ALU.mult).then_inc(sem["probs"], 1)
                    if t == 1 and not last:
                        ln_scale(g + 1)
                    if t == 2 and not last:
                        ln_rows(g + 1, (u + 1) % GPS, (0, 1))
                if not last:
                    ln_rows(g + 1, (u + 1) % GPS, (2, 3))
                for c in (2, 3):
                    wait(pool, "mix", g, c - 2)
                    xf(g, c)

            def xf(g, c):
                pool.tensor_tensor(xf_b[c % 2][:, :], xT_h[:, c, :].bitcast(F32), xT_l[:, c, :].bitcast(F32),
                                   ALU.add).then_inc(sem["xf"], 1)
            loop(pool, body)

        @block.scalar
        def _(act):
            credit(act, BY_ACT)

            def xT_hi(g):
                for t in range(T):
                    wait(act, "xT_ps", g, t)
                    if t == 0:
                        wait(act, "xf", g - 1, KB - 1)
                        wait(act, "gate_ps", g - 1, KB - 1)
                    act.activation(xT_h[:, :, t * P:(t + 1) * P], ps(f"xT{t}")[:, :].rearrange("p (k n) -> p k n", k=KB),
                                   ACT.Copy).then_inc(sem["xT_hi"], 1)

            xT_hi(0)

            def nT_hi(g, t):
                wait(act, "nT_ps", g, t)
                if t < 2:
                    wait(act, "num_ps", g, t + 2)
                else:
                    wait(act, "out_ps", g, t - 2)
                act.activation(nT_h[:, t % 2, :], ps(f"nT{t}")[:, :], ACT.Copy).then_inc(sem["nT_hi"], 1)

            def v_hi(g, t):
                wait(act, "v_ps", g, t)
                if t < 2:
                    wait(act, "out_ps", g - 1, t + 2)
                else:
                    wait(act, "num_ps", g, t - 2)
                act.activation(v_h[:, t % 2, :], ps(f"v{t}")[:, :], ACT.Copy).then_inc(sem["v_hi"], 1)

            def body(g, u, i, last):
                wait(act, "c1_ps", g)
                wait(act, "mix_lo", g - 1, KB - 1)
                act.activation(c1s[:, :], ps("c1")[:, :], ACT.Sigmoid, bias=c1b[:, 0:1]).then_inc(sem["c1_sig"], 1)
                wait(act, "f_clip", g)
                act.activation(ef[:, :], ef[:, :], ACT.Exp, scale=-1.0).then_inc(sem["f_exp"], 1)
                wait(act, "qk_min", g)
                act.activation(qk[:, :], qk[:, :], ACT.Exp).then_inc(sem["qk_exp"], 1)
                wait(act, "u", g)
                act.activation(ef[:, :], ef[:, :], ACT.Ln).then_inc(sem["ln_u"], 1)
                wait(act, "l_clip", g)
                act.activation(dec[:, :], dec[:, :], ACT.Exp, scale=sign[:, 0:1]).then_inc(sem["decay"], 1)
                wait(act, "es_sub", g, 1)
                act.activation(flat(sx[:, 0:2, :]), flat(sx[:, 0:2, :]), ACT.Exp).then_inc(sem["es_exp"], 1)
                wait(act, "q_dup", g, 1)
                wait(act, "ret_ps", g - 1, KB - 1)
                act.activation(q2_h[:, :], q2[:, :], ACT.Copy).then_inc(sem["q_hi"], 1)
                wait(act, "k_dec", g)
                wait(act, "a_ps", g - 1)
                act.activation(k_hl[0:M, :], kf[:, :], ACT.Copy).then_inc(sem["k_hi"], 1)
                act.activation(kh[:, :], kf[:, :], ACT.Copy).then_inc(sem["k_hi"], 1)
                wait(act, "es_sub", g, 3)
                act.activation(flat(sx[:, 2:4, :]), flat(sx[:, 2:4, :]), ACT.Exp).then_inc(sem["es_exp"], 1)
                v_hi(g, 0)
                v_hi(g, 1)
                wait(act, "kT_ps", g)
                wait(act, "state_ps", g - 1, T - 1)
                act.activation(flat(kT_hl[:, :, :]), ps("kT")[:, :], ACT.Copy).then_inc(sem["kT_sb"], 1)
                wait(act, "a_mask", g)
                wait(act, "out_ps", g - 1, T - 1)
                act.activation(a_h[:, :], am[:, :], ACT.Copy).then_inc(sem["a_hi"], 1)
                wait(act, "lg_sub", g)
                act.activation(flat(lg[:, :, :]), flat(lg[:, :, :]), ACT.Exp).then_inc(sem["w_exp"], 1)
                gate_sig(g, 0)
                for t in range(2):
                    s_hi(g, t)
                    v_hi(g, t + 2)
                    n_rows(g, t)
                s_hi(g, 2)
                nT_hi(g, 0)
                gate_sig(g, 1)
                n_rows(g, 2)
                wait(act, "sT_ps", g)
                act.activation(sT_h[:, :], ps("sT")[:, :], ACT.Copy).then_inc(sem["sT_hi"], 1)
                nT_hi(g, 1)
                wait(act, "aT_ps", g)
                act.activation(aT_h[:, :], ps("aT")[:, :], ACT.Copy).then_inc(sem["aT_hi"], 1)
                n_rows(g, 3)
                s_hi(g, 3)
                gate_sig(g, 2)
                mix_hi(g, 0)
                mix_hi(g, 1)
                gate_sig(g, 3)
                mix_hi(g, 2)
                mix_hi(g, 3)
                nT_hi(g, 2)
                nT_hi(g, 3)
                if not last:
                    xT_hi(g + 1)

            def s_hi(g, t):
                wait(act, "state_ps", g, t)
                act.activation(s_h[:, :], state[:, :], ACT.Copy).then_inc(sem["s_hi"], 1)

            def n_rows(g, t):
                wait(act, "n_bias", g, t)
                if t >= 2:
                    wait(act, "nT_ps", g, t - 2)
                else:
                    wait(act, "nT_ps", g - 1, t + 2)
                act.activation(n[:, t % 2, :], ps(f"num{t}")[:, :], ACT.Identity, bias=nbi[:, t:t + 1],
                               scale=nsc[:, t:t + 1]).then_inc(sem["n_rows"], 1)

            def gate_sig(g, c):
                wait(act, "gate_ps", g, c)
                if c >= 2:
                    wait(act, "mix_mul", g, c - 2)
                act.activation(gate_b[c % 2][:, :], ps(f"gate{c}")[:, :], ACT.Sigmoid,
                               bias=sgb[:, c:c + 1]).then_inc(sem["gate"], 1)

            def mix_hi(g, c):
                wait(act, "mix", g, c)
                if c == 0:
                    wait(act, "so_ps", g - 1, T - 1)
                act.activation(mixT_h[:, c, :], mix_b[c % 2][:, :], ACT.Copy).then_inc(sem["mix_hi"], 1)
            loop(act, body)

        @block.tensor
        def _(pe):
            credit(pe, BY_PE)

            def xT(g, slot):
                for t in range(T):
                    wait(pe, "xn_rows", g, t)
                    bank_free(pe, f"xT{t}", slot)
                    for k in range(KB):
                        last = pe.transpose(ps(f"xT{t}")[:, k * P:(k + 1) * P], xn[:, t, k * P:(k + 1) * P],
                                            ident[:, :])
                    last.then_inc(sem["xT_ps"], 1)

            def by_feature(g, use, signal, wh, wl):
                bank_free(pe, use, g)
                for k in range(KB):
                    last = split3(pe, ps(use)[:, :], wh(k), wl(k), xT_h[:, k, :], xT_l[:, k, :], k == 0, k == KB - 1)
                last.then_inc(sem[signal], 1)

            def v_rows(g, t):
                bank_free(pe, f"v{t}", g)
                for k in range(KB):
                    last = split3(pe, ps(f"v{t}")[:, :], xT_h[:, k, t * P:(t + 1) * P], xT_l[:, k, t * P:(t + 1) * P],
                                  wv_h[:, k, :], wv_l[:, k, :], k == 0, k == KB - 1)
                last.then_inc(sem["v_ps"], 1)

            def nT(g, t):
                wait(pe, "n_rows", g, t)
                bank_free(pe, f"nT{t}", g)
                for k in range(KB):
                    last = pe.transpose(ps(f"nT{t}")[:, k * P:(k + 1) * P], n[:, t % 2, k * P:(k + 1) * P], ident[:, :])
                last.then_inc(sem["nT_ps"], 1)

            def out_rows(g, t):
                wait(pe, "nT_lo", g, t)
                bank_free(pe, f"out{t}", g)
                o = ps(f"out{t}")[:, :]
                cols = slice(t * P, (t + 1) * P)
                split3(pe, o, aT_h[:, cols], aT_l[:, cols], wve_h[:, :], wve_l[:, :], True, False)
                for k in range(KB):
                    blk = slice(k * P, (k + 1) * P)
                    last = split3(pe, o, nT_h[:, t % 2, blk], nT_l[:, t % 2, blk], wwo_h[:, k, :], wwo_l[:, k, :],
                                  False, k == KB - 1)
                last.then_inc(sem["out_ps"], 1)

            xT(0, -1)

            def body(g, u, i, last_group):
                wait(pe, "xT_lo", g, T - 1)
                by_feature(g, "c1", "c1_ps", lambda k: wc1_h[:, k, :], lambda k: wc1_l[:, k, :])
                by_feature(g, "f", "f_ps", lambda k: wqkf_h[:, k, 2 * M:], lambda k: wqkf_l[:, k, 2 * M:])
                by_feature(g, "qk", "qk_ps", lambda k: wqkf_h[:, k, 0:2 * M], lambda k: wqkf_l[:, k, 0:2 * M])
                for b in range(2):
                    bank_free(pe, f"es{b}", g)
                    for j in range(2):
                        t = 2 * b + j
                        for k in range(KB):
                            last = split3(pe, ps(f"es{b}")[:, j * WES:(j + 1) * WES], xT_h[:, k, t * P:(t + 1) * P],
                                          xT_l[:, k, t * P:(t + 1) * P], wes_h[:, k, :], wes_l[:, k, :],
                                          k == 0, k == KB - 1)
                    last.then_inc(sem["es_ps"], 1)
                v_rows(g, 0)
                v_rows(g, 1)
                wait(pe, "k_lo", g)
                bank_free(pe, "kT", g)
                for t in range(T):
                    last = pe.transpose(ps("kT")[:, t * P:(t + 1) * P], k_hl[:, t * P:(t + 1) * P].bitcast(F32), ident[:, :])
                last.then_inc(sem["kT_ps"], 1)
                wait(pe, "q_lo", g)
                bank_free(pe, "a", g)
                for t in range(T):
                    cols = slice(t * P, (t + 1) * P)
                    pe.matmul(ps("a")[:, cols], k_hl[:, cols], q2_h[:, cols], start=True, stop=False)
                    last = pe.matmul(ps("a")[:, cols], k_hl[:, cols], q2_l[:, cols], start=False, stop=True)
                last.then_inc(sem["a_ps"], 1)
                wait(pe, "silu", g)
                wait(pe, "qz", g)
                bank_free(pe, "small", g)
                for t in range(T):
                    pe.matmul(ps("small")[:, 4 * t:4 * t + 3], c1s[:, t * P:(t + 1) * P], c2w[:, :], start=True, stop=True)
                    last = pe.matmul(ps("small")[:, 4 * t + 3:4 * t + 4], zc[:, t * P:(t + 1) * P], ones[0:M, :],
                                     start=True, stop=True)
                last.then_inc(sem["small_ps"], 1)

                def gate(c):
                    blk = slice(c * P, (c + 1) * P)
                    by_feature(g, f"gate{c}", "gate_ps", lambda k: wsg_h[:, k, blk], lambda k: wsg_l[:, k, blk])

                def retrieved(c):
                    blk = slice(c * P, (c + 1) * P)
                    bank_free(pe, f"ret{c}", g)
                    pe.matmul(ps(f"ret{c}")[:, :], know_hl[:, blk], sT_h[:, :], start=True, stop=False)
                    pe.matmul(ps(f"ret{c}")[:, :], know_hl[:, blk], sT_l[:, :], start=False, stop=True)\
                        .then_inc(sem["ret_ps"], 1)

                gate(0)
                for t in range(T):
                    cols = slice(t * P, (t + 1) * P)
                    o = ps(f"num{t}")[:, :]
                    bank_free(pe, f"num{t}", g)
                    first = u == 0 and t == 0
                    if not first:
                        wait(pe, "s_lo", g if t else g - 1, t - 1 if t else T - 1)
                        split3(pe, o, q2_h[:, cols], q2_l[:, cols], s_h[:, :], s_l[:, :], True, False)
                    wait(pe, "kT_sb", g)
                    wait(pe, "v_lo", g, t)
                    if first:
                        wait(pe, "s_lo", g - 1, T - 1)
                    pe.matmul(state[:, :], kT_hl[:, t, :], v_h[:, t % 2, :], start=first, stop=False, skip_group_check=True)
                    pe.matmul(state[:, :], kT_hl[:, t, :], v_l[:, t % 2, :], start=False, stop=True,
                              skip_group_check=True).then_inc(sem["state_ps"], 1)
                    if t == 0:
                        wait(pe, "a_lo", g)
                    split3(pe, o, a_h[:, cols], a_l[:, cols], v_h[:, t % 2, :], v_l[:, t % 2, :], first, True)\
                        .then_inc(sem["num_ps"], 1)
                    if t < 2:
                        v_rows(g, t + 2)
                    elif t == 2:
                        nT(g, 0)
                        gate(1)
                        nT(g, 1)
                wait(pe, "probs", g, 2)
                bank_free(pe, "sT", g)
                for t in range(T):
                    last = pe.transpose(ps("sT")[:, t * P:(t + 1) * P], pr[:, t, P:2 * P], ident[:, :])
                last.then_inc(sem["sT_ps"], 1)
                bank_free(pe, "aT", g)
                for t in range(T):
                    last = pe.transpose(ps("aT")[:, t * P:(t + 1) * P], pr[:, t, 0:P], ident[:, :])
                last.then_inc(sem["aT_ps"], 1)
                gate(2)
                wait(pe, "sT_lo", g)
                retrieved(0)
                retrieved(1)
                gate(3)
                retrieved(2)
                retrieved(3)
                wait(pe, "aT_lo", g)
                out_rows(g, 0)
                nT(g, 2)
                out_rows(g, 1)
                nT(g, 3)
                wait(pe, "mix_lo", g, KB - 1)
                for t in range(T):
                    cols = slice(t * P, (t + 1) * P)
                    bank_free(pe, f"so{t}", g)
                    for k in range(KB):
                        last = split3(pe, ps(f"so{t}")[:, :], mixT_h[:, k, cols], mixT_l[:, k, cols], wso_h[:, k, :],
                                      wso_l[:, k, :], k == 0, k == KB - 1)
                    last.then_inc(sem["so_ps"], 1)
                if not last_group:
                    xT(g + 1, g)
                out_rows(g, 2)
                out_rows(g, 3)
            loop(pe, body)

        @block.vector
        def _(dve):
            credit(dve, BY_DVE)

            def done(ins, name):
                ins.then_inc(sem[name], 1)

            def ln_stats(g, u, tiles):
                for t in tiles:
                    wait(dve, f"h_in{t}", g)
                    if t == 0:
                        wait(dve, "ln_var", g - 1)
                        wait(dve, "ln_bias", g - 1)
                    done(dve.bn_stats(bn6[:, t, :], h[u][:, t, :]), "ln_bn")
                for t in tiles:
                    wait(dve, "ln_bn", g, t)
                    waits_end(dve)
                    done(dve.bn_aggr(mv[:, t, :], bn6[:, t, :]), "ln_stats")

            def ln_bias(g):
                wait(dve, "ln_rstd", g)
                wait(dve, "xn_rows", g - 1, T - 1)
                done(dve.scalar_tensor_tensor(nmr[:, :], mv[:, :, 0], -1.0, rstd[:, :], ALU.mult, ALU.mult), "ln_bias")

            def xT_lo(g):
                for t in range(T):
                    wait(dve, "xT_hi", g, t)
                    cols = slice(t * P, (t + 1) * P)
                    done(dve.tensor_tensor(xT_l[:, :, cols], ps(f"xT{t}")[:, :].rearrange("p (k n) -> p k n", k=KB),
                                           xT_h[:, :, cols].bitcast(F32), ALU.subtract), "xT_lo")

            def v_lo(g, t):
                wait(dve, "v_hi", g, t)
                done(dve.tensor_tensor(v_l[:, t % 2, :], ps(f"v{t}")[:, :], v_h[:, t % 2, :].bitcast(F32),
                                       ALU.subtract), "v_lo")

            def nT_lo(g, t):
                wait(dve, "nT_hi", g, t)
                done(dve.tensor_tensor(nT_l[:, t % 2, :], ps(f"nT{t}")[:, :], nT_h[:, t % 2, :].bitcast(F32),
                                       ALU.subtract), "nT_lo")

            def es(g, b):
                two = slice(2 * b, 2 * b + 2)
                e2 = ps(f"es{b}")[:, 0:2 * WES].rearrange("p (t n) -> p t n", t=2)
                eE = e2[:, :, 0:HS].rearrange("p t (h s) -> p t h s", h=H)
                wait(dve, "es_ps", g, b)
                done(dve.tensor_reduce(mE[:, two, :], eE, AX.X, ALU.max), "es_max")
                done(dve.tensor_reduce(mS[:, two], e2[:, :, HS:WES], AX.X, ALU.max), "es_max")
                if b == 0:
                    wait(dve, "probs", g - 1, 2)
                wait(dve, "es_max", g, 2 * b)
                done(dve.tensor_tensor(sx[:, two, 0:HS].rearrange("p t (h s) -> p t h s", h=H), eE,
                                       mE[:, two, :].unsqueeze(3).to_broadcast([P, 2, H, SE]), ALU.subtract), "es_sub")
                wait(dve, "es_max", g, 2 * b + 1)
                done(dve.tensor_tensor(sx[:, two, HS:WES], e2[:, :, HS:WES],
                                       mS[:, two].unsqueeze(2).to_broadcast([P, 2, SS]), ALU.subtract), "es_sub")

            def body(g, u, i, last):
                wait(dve, "c1_sig", g)
                done(dve.scalar_tensor_tensor(c1s[:, :], ps("c1")[:, :], c1b[:, 0:1], c1s[:, :], ALU.add, ALU.mult), "silu")
                wait(dve, "f_ps", g)
                wait(dve, "mix_mul", g - 1, KB - 1)
                done(dve.tensor_scalar(ef[:, :], ps("f")[:, :], bff[:, 0:1], F_CLIP, ALU.add, ALU.max), "f_clip")
                wait(dve, "qk_ps", g)
                wait(dve, "mix_lo", g - 1, KB - 1)
                done(dve.tensor_scalar(qk[:, :], ps("qk")[:, :], 0.0, None, ALU.min), "qk_min")
                wait(dve, "f_exp", g)
                done(dve.tensor_scalar(ef[:, :], ef[:, :], 1.0, 1.0 / FORGET_MIN, ALU.add, ALU.min), "u")
                wait(dve, "qk_exp", g)
                done(dve.scalar_tensor_tensor(qk[:, :], ps("qk")[:, :], 0.0, qk[:, :], ALU.max, ALU.add), "qk_elu")
                wait(dve, "ln_u", g)
                wait(dve, "l_carry", g - 1)
                done(dve.tensor_tensor_scan(lraw[:, :], ones[:, :].to_broadcast([P, GT]), ef[:, :],
                                            carry[:, 0:1] if u else 0.0, ALU.mult, ALU.subtract), "lsum_raw")
                wait(dve, "lsum_raw", g)
                done(dve.tensor_scalar(dec[:, :], lraw[:, :], -LOG_CLIP, LOG_CLIP, ALU.max, ALU.min), "l_clip")
                done(dve.tensor_copy(carry[:, 0:1], lraw[:, GT - 1:GT]), "l_carry")
                es(g, 0)
                wait(dve, "decay", g)
                wait(dve, "qk_elu", g)
                wait(dve, "q_lo", g - 1)
                for z in range(2):
                    done(dve.scalar_tensor_tensor(q2[z * M:(z + 1) * M, :], qk[0:M, :], Q_SCALE, dec[0:M, :], ALU.mult,
                                                  ALU.mult), "q_dup")
                wait(dve, "k_lo", g - 1)
                done(dve.tensor_tensor(kf[:, :], qk[M:2 * M, :], dec[M:2 * M, :], ALU.mult), "k_dec")
                wait(dve, "k_dec", g)
                wait(dve, "small_ps", g - 1)
                wait(dve, "z_carry", g - 1)
                done(dve.tensor_tensor_scan(zc[:, :], ones[0:M, :].to_broadcast([M, GT]), kf[:, :],
                                            carry[0:M, 1:2] if u else 0.0, ALU.mult, ALU.add), "z_sum")
                wait(dve, "z_sum", g)
                done(dve.tensor_copy(carry[0:M, 1:2], zc[:, GT - 1:GT]), "z_carry")
                wait(dve, "k_hi", g, 1)
                done(dve.tensor_tensor(k_hl[M:2 * M, :], kf[:, :], kh[:, :].bitcast(F32), ALU.subtract), "k_lo")
                wait(dve, "q_hi", g)
                done(dve.tensor_tensor(q2_l[:, :], q2[:, :], q2_h[:, :].bitcast(F32), ALU.subtract), "q_lo")
                wait(dve, "z_carry", g)
                wait(dve, "q_dup", g, 0)
                done(dve.tensor_tensor(zc[:, :], zc[:, :], q2[0:M, :], ALU.mult), "qz")
                es(g, 1)
                v_lo(g, 0)
                wait(dve, "a_ps", g)
                done(dve.tensor_tensor(am[:, :].rearrange("p (t n) -> p t n", t=T),
                                       ps("a")[:, :].rearrange("p (t n) -> p t n", t=T),
                                       causal[:, :].unsqueeze(1).to_broadcast([P, T, P]), ALU.mult), "a_mask")
                v_lo(g, 1)
                wait(dve, "a_hi", g)
                done(dve.tensor_tensor(a_l[:, :], am[:, :], a_h[:, :].bitcast(F32), ALU.subtract), "a_lo")
                wait(dve, "es_exp", g, 1)
                done(dve.tensor_reduce(rs[:, :, 0:H], sx[:, :, 0:HS].rearrange("p t (h s) -> p t h s", h=H), AX.X,
                                       ALU.add), "es_sum")
                done(dve.tensor_reduce(rs[:, :, H], sx[:, :, HS:WES], AX.X, ALU.add), "es_sum")
                wait(dve, "es_sum", g, 1)
                done(dve.reciprocal(flat(rs[:, :, :]), flat(rs[:, :, :])), "es_rec")
                wait(dve, "small_ps", g)
                small = ps("small")[:, 0:4 * T].rearrange("p (t n) -> p t n", t=T)
                done(dve.tensor_tensor(lg[:, :, :], small[:, :, 0:3], c2b[:, :].unsqueeze(1).to_broadcast([P, T, 3]),
                                       ALU.add), "lg_add")
                done(dve.tensor_scalar(den[:, :], small[:, :, 3], DEN_EPS, None, ALU.add), "den_add")
                wait(dve, "lg_add", g)
                done(dve.tensor_reduce(lm[:, :], lg[:, :, :], AX.X, ALU.max), "lg_max")
                wait(dve, "den_add", g)
                done(dve.reciprocal(den[:, :], den[:, :]), "den_rec")
                wait(dve, "lg_max", g)
                done(dve.tensor_tensor(lg[:, :, :], lg[:, :, :], lm[:, :].unsqueeze(2).to_broadcast([P, T, 3]),
                                       ALU.subtract), "lg_sub")
                wait(dve, "den_rec", g)
                done(dve.tensor_tensor(den2[:, :], den[:, :], den[:, :], ALU.mult), "den_sq")
                wait(dve, "w_exp", g)
                done(dve.tensor_reduce(lsum[:, :], lg[:, :, :], AX.X, ALU.add), "w_sum")
                wait(dve, "w_sum", g)
                done(dve.reciprocal(lsum[:, :], lsum[:, :]), "w_rec")
                wait(dve, "w_rec", g)
                done(dve.tensor_tensor(w[:, :, :], lg[:, :, :], lsum[:, :].unsqueeze(2).to_broadcast([P, T, 3]),
                                       ALU.mult), "w_done")
                wait(dve, "w_done", g)
                wait(dve, "es_rec", g)
                done(dve.tensor_tensor(rs[:, :, 0:H], rs[:, :, 0:H], w[:, :, 1:2].to_broadcast([P, T, H]), ALU.mult), "rE_w")
                done(dve.tensor_tensor(rdw[:, :], den[:, :], w[:, :, 0], ALU.mult), "rd_w")
                for t in range(T):
                    if t < 3:
                        s_lo(g, t)
                    wait(dve, "num_ps", g, t)
                    done(dve.bn_stats(nb6[:, t, :], ps(f"num{t}")[:, :]), "n_bn")
                    wait(dve, "n_bn", g, t)
                    waits_end(dve)
                    done(dve.bn_aggr(nmv[:, t, :], nb6[:, t, :]), "n_stats")
                    wait(dve, "n_stats", g, t)
                    wait(dve, "den_sq", g)
                    done(dve.tensor_scalar(nv[:, t:t + 1], nmv[:, t, 1:2], den2[:, t:t + 1], LN_EPS, ALU.mult, ALU.add),
                         "n_var")
                    if t < 2:
                        v_lo(g, t + 2)
                    elif t == 2:
                        nT_lo(g, 0)
                    else:
                        wait(dve, "sT_hi", g)
                        done(dve.tensor_tensor(sT_l[:, :], ps("sT")[:, :], sT_h[:, :].bitcast(F32), ALU.subtract), "sT_lo")
                    wait(dve, "n_rstd", g, t)
                    wait(dve, "rd_w", g)
                    done(dve.tensor_tensor(nsc[:, t:t + 1], nrs[:, t:t + 1], rdw[:, t:t + 1], ALU.mult), "n_scale")
                    wait(dve, "n_scale", g, t)
                    done(dve.scalar_tensor_tensor(nbi[:, t:t + 1], nmv[:, t, 0:1], -1.0, nsc[:, t:t + 1], ALU.mult,
                                                  ALU.mult), "n_bias")
                    if t < 2 and not last:
                        ln_stats(g + 1, (u + 1) % GPS, (2 * t, 2 * t + 1))
                    if t == 2:
                        if not last:
                            ln_bias(g + 1)
                        for r in range(T):
                            done(dve.scalar_tensor_tensor(h[u][:, r, :], bias_wo[:, :], w[:, r, 0:1], h[u][:, r, :],
                                                          ALU.mult, ALU.add), "h_bias")
                        xg(g, 0)
                nT_lo(g, 1)
                wait(dve, "aT_hi", g)
                done(dve.tensor_tensor(aT_l[:, :], ps("aT")[:, :], aT_h[:, :].bitcast(F32), ALU.subtract), "aT_lo")
                xg(g, 1)
                s_lo(g, 3)
                mix_mul(g, 0)
                mix(g, 0)
                mix_mul(g, 1)
                mix(g, 1)
                mix_lo(g, 0)
                xg(g, 2)
                mix_mul(g, 2)
                mix_lo(g, 1)
                mix(g, 2)
                xg(g, 3)
                mix_mul(g, 3)
                mix_lo(g, 2)
                mix(g, 3)
                mix_lo(g, 3)
                h_out(g, u, 0)
                nT_lo(g, 2)
                h_out(g, u, 1)
                nT_lo(g, 3)
                for t in range(T):
                    h_so(g, u, t)
                if not last:
                    xT_lo(g + 1)
                h_out(g, u, 2)
                h_out(g, u, 3)

            def s_lo(g, t):
                wait(dve, "s_hi", g, t)
                done(dve.tensor_tensor(s_l[:, :], state[:, :], s_h[:, :].bitcast(F32), ALU.subtract), "s_lo")

            def xg(g, c):
                wait(dve, "xf", g, c)
                wait(dve, "gate", g, c)
                done(dve.scalar_tensor_tensor(xf_b[c % 2][:, :], gate_b[c % 2][:, :], 1.0, xf_b[c % 2][:, :],
                                              ALU.subtract, ALU.mult), "xg")

            def mix_mul(g, c):
                wait(dve, "ret_ps", g, c)
                wait(dve, "gate", g, c)
                if c >= 2:
                    wait(dve, "mix_lo", g, c - 2)
                done(dve.tensor_tensor(mix_b[c % 2][:, :], ps(f"ret{c}")[:, :], gate_b[c % 2][:, :], ALU.mult), "mix_mul")

            def mix(g, c):
                wait(dve, "mix_mul", g, c)
                wait(dve, "xg", g, c)
                done(dve.tensor_tensor(mix_b[c % 2][:, :], mix_b[c % 2][:, :], xf_b[c % 2][:, :], ALU.subtract), "mix")

            def mix_lo(g, c):
                wait(dve, "mix_hi", g, c)
                done(dve.tensor_tensor(mixT_l[:, c, :], mix_b[c % 2][:, :], mixT_h[:, c, :].bitcast(F32), ALU.subtract),
                     "mix_lo")

            def h_so(g, u, t):
                wait(dve, "so_ps", g, t)
                if t < 2:
                    wait(dve, "h_out", g, t)
                else:
                    wait(dve, "h_bias", g, t)
                done(dve.scalar_tensor_tensor(h[u][:, t, :], ps(f"so{t}")[:, :], w[:, t, 2:3], h[u][:, t, :],
                                              ALU.mult, ALU.add), "h_so")

            def h_out(g, u, t):
                wait(dve, "out_ps", g, t)
                if t < 2:
                    wait(dve, "h_bias", g, t)
                else:
                    wait(dve, "h_so", g, t)
                done(dve.tensor_tensor(h[u][:, t, :], ps(f"out{t}")[:, :], h[u][:, t, :], ALU.add), "h_out")

            ln_stats(0, 0, range(T))
            ln_bias(0)
            xT_lo(0)
            loop(dve, body)


def prep_a(nc, e, r):
    bank, ident, half, blocks = e["bank"], e["ident"], e["half"], e["blocks"]
    (D, KB, M, SE, SS, H, HD, HS, WES) = (r.get(n, e.get(n)) for n in ("D", "KB", "M", "SE", "SS", "H", "HD", "HS", "WES"))
    know_hl, ones = r["know_hl"], r["ones"]
    with nc.cleanup_on_exit(), ExitStack() as ctx:
        def sb(name, shape, dt=F32):
            return ctx.enter_context(nc.sbuf_tensor(name, shape, dt))

        def new(name):
            return nc.alloc_semaphore("PA_" + name)

        raw = {n: sb("raw_" + n, [P, KB, D]) for n in ("Eq", "Sin", "Ek", "Ev", "Eo", "Wo", "Wv", "Sg_w", "So")}
        raw_qkf, raw_c1 = sb("raw_qkf", [P, KB, 4 * M]), sb("raw_c1", [P, KB, P])
        raw_es, raw_kn = sb("raw_es", [SE, D]), sb("raw_kn", [P, D])
        EqT, SinT = sb("EqT", [P, H, D]), sb("SinT", [P, KB, D])
        esT, knT = sb("esT", [P, KB, SE]), sb("knT", [P, KB, SS])
        khT = sb("khT", [P, H, SE])
        vhT = sb("vhT", [P, H, HS])
        wes, wve = sb("wes", [P, KB, WES]), sb("wve", [P, D])
        kn_hi = sb("kn_hi", [P, D], F32R)
        lng, lnb, lnb_w = sb("lng", [P, KB]), sb("lnb", [P, KB]), sb("lnb_w", [P, KB, P])
        one_mat = sb("one_mat", [P, P])

        loads = {n: new("in_" + n) for n in ("Eq", "Sin", "Ek", "Ev", "Eo", "Wo", "Wv", "Sg_w", "So", "qkf", "c1", "es",
                                             "kn", "ln", "small")}
        zeroed, ident_ok, causal_ok = new("zeroed"), new("ident_ok"), new("causal_ok")
        small_T, small_sb = new("small_T"), new("small_sb")
        big_T, big_sb = new("big_T"), new("big_sb")
        heads, heads_sb = new("heads"), new("heads_sb")
        folded, folded_sb = new("folded"), new("folded_sb")
        lnb_sb, wo_row, wo_row_sb, wo_g = new("lnb_sb"), new("wo_row"), new("wo_row_sb"), new("wo_g")
        hi, lo = new("hi"), new("lo")
        kn_split, signed = new("kn_split"), new("signed")

        SPLITS = [("Wv", loads["Wv"], 16, raw["Wv"], r["wv_h"], r["wv_l"]),
                  ("Sg_w", loads["Sg_w"], 16, raw["Sg_w"], r["wsg_h"], r["wsg_l"]),
                  ("So", loads["So"], 16, raw["So"], r["wso_h"], r["wso_l"]),
                  ("qkf", loads["qkf"], 64, raw_qkf, r["wqkf_h"], r["wqkf_l"]),
                  ("c1", loads["c1"], 16, raw_c1, r["wc1_h"], r["wc1_l"]),
                  ("Wo", wo_g, KB, raw["Wo"], r["wwo_h"], r["wwo_l"]),
                  ("wes", folded_sb, 2, wes, r["wes_h"], r["wes_l"]),
                  ("wve", folded_sb, 3, wve, r["wve_h"], r["wve_l"])]

        block = ctx.enter_context(nc.Block())

        @block.sync
        def _(sp):
            sp.dma_start(raw_es[:, :], e["eslots"][0]).then_inc(loads["es"], 16)
            sp.dma_start(raw_kn[0:SS, :], e["know"][0]).then_inc(loads["kn"], 16)
            sp.dma_start(raw_kn[SS:2 * SS, :], e["know"][0]).then_inc(loads["kn"], 16)
            for n in ("Ek", "Ev", "Eo", "Wv", "So"):
                sp.dma_start(raw[n][:, :, :], blocks(e[n])).then_inc(loads[n], 16)
            for j, n in enumerate(("Wq", "Wk", "Wf", "Wf")):
                sp.dma_start(raw_qkf[:, :, j * M:(j + 1) * M], blocks(e[n])).then_inc(loads["qkf"], 16)

        @block.scalar
        def _(act):
            for n in ("Eq", "Sin", "Wo", "Sg_w"):
                act.dma_start(raw[n][:, :, :], blocks(e[n])).then_inc(loads[n], 16)
            act.dma_start(raw_c1[:, :, :], blocks(e["C1w"])).then_inc(loads["c1"], 16)
            for j in range(2 * KB):
                act.wait_ge(big_T, j + 1)
                dst = (EqT if j < KB else SinT)[:, j % KB, :]
                act.activation(dst, bank[j % 4][:, :], ACT.Copy).then_inc(big_sb, 1)
            act.wait_ge(heads, 1)
            act.activation(khT[:, :, :].rearrange("p h s -> p (h s)"), bank[4][:, 0:HS], ACT.Copy).then_inc(heads_sb, 1)
            act.wait_ge(folded, 1)
            act.activation(wes[:, :, 0:HS], bank[5][:, 0:KB * HS].rearrange("p (k n) -> p k n", k=KB), ACT.Copy,
                           scale=float(HD) ** -0.5).then_inc(folded_sb, 1)
            act.wait_ge(folded, 2)
            act.activation(wes[:, :, HS:WES], bank[6][:, 0:KB * SS].rearrange("p (k n) -> p k n", k=KB), ACT.Copy,
                           scale=float(D) ** -0.5).then_inc(folded_sb, 1)
            act.wait_ge(folded, 3)
            act.activation(wve[:, :], bank[7][:, :], ACT.Copy).then_inc(folded_sb, 1)
            for _, ready, value, full, hi_t, _ in SPLITS:
                act.wait_ge(ready, value)
                act.activation(hi_t[:], full[:], ACT.Copy).then_inc(hi, 1)

        @block.gpsimd
        def _(pool):
            for a, v in ((ident, 0.0), (one_mat, 1.0), (half, -0.5), (ones, 1.0), (vhT, 0.0)):
                pool.memset(a[:], v).then_inc(zeroed, 1)
            pool.wait_ge(zeroed, 5)
            pool.affine_select(out=ident[:, :], in_=ident[:, :], compare_op=ALU.not_equal, fill=1.0, base=0,
                               pattern=[[-1, P]], channel_multiplier=1).then_inc(ident_ok, 1)
            pool.affine_select(out=r["causal"][:, :], in_=one_mat[:, :], compare_op=ALU.is_ge, fill=0.0, base=0,
                               pattern=[[1, P]], channel_multiplier=-1).then_inc(causal_ok, 1)
            pool.dma_start(lng[:, :], e["ln_g"].rearrange("(k p) -> p k", p=P), allow_slow_non_contiguous=True).then_inc(loads["ln"], 16)
            pool.dma_start(lnb[:, :], e["ln_b"].rearrange("(k p) -> p k", p=P), allow_slow_non_contiguous=True).then_inc(loads["ln"], 16)
            pool.dma_start(r["c1b"][:, :], e["C1b"].rearrange("(p a) -> p a", a=1), allow_slow_non_contiguous=True).then_inc(loads["small"], 16)
            pool.dma_start(r["sgb"][:, :], e["Sg_b"].rearrange("(k p) -> p k", p=P), allow_slow_non_contiguous=True).then_inc(loads["small"], 16)
            pool.dma_start(r["c2w"][:, :], e["C2w"]).then_inc(loads["small"], 16)
            pool.dma_start(r["c2b"][:, :], e["C2b"].rearrange("(a n) -> a n", a=1).to_broadcast([P, 3])).then_inc(loads["small"], 16)
            for z in range(2):
                pool.dma_start(r["bff"][z * M:(z + 1) * M, :], e["bf"].rearrange("(p a) -> p a", a=1), allow_slow_non_contiguous=True).then_inc(loads["small"], 16)
            pool.wait_ge(loads["small"], 96)

        @block.tensor
        def _(pe):
            pe.wait_ge(ident_ok, 1)
            pe.wait_ge(loads["es"], 16)
            for k in range(KB):
                last = pe.transpose(bank[4][:, k * SE:(k + 1) * SE], raw_es[:, k * P:(k + 1) * P], ident[0:SE, 0:SE])
            last.then_inc(small_T, 1)
            pe.wait_ge(loads["kn"], 32)
            for k in range(KB):
                last = pe.transpose(bank[5][:, k * SS:(k + 1) * SS], raw_kn[0:SS, k * P:(k + 1) * P], ident[0:SS, 0:SS])
            last.then_inc(small_T, 1)
            for j in range(2 * KB):
                n, blk = ("Eq", j) if j < KB else ("Sin", j - KB)
                pe.wait_ge(loads[n], 16)
                if j >= 4:
                    pe.wait_ge(big_sb, j - 3)
                for k in range(KB):
                    last = pe.transpose(bank[j % 4][:, k * P:(k + 1) * P], raw[n][:, k, blk * P:(blk + 1) * P], ident[:, :])
                last.then_inc(big_T, 1)
            pe.wait_ge(small_sb, 2)
            for n, o in (("Ek", bank[4]), ("Ev", bank[5])):
                pe.wait_ge(loads[n], 16)
                for hd in range(H):
                    for k in range(KB):
                        last = pe.matmul(o[:, hd * SE:(hd + 1) * SE], raw[n][:, k, hd * HD:(hd + 1) * HD], esT[:, k, :],
                                         start=k == 0, stop=k == KB - 1)
                last.then_inc(heads, 1)
            pe.wait_ge(lnb_sb, 1)
            pe.wait_ge(loads["Wo"], 16)
            pe.wait_ge(big_sb, 2 * KB)
            for k in range(KB):
                last = pe.matmul(bank[0][:, :], lnb_w[:, k, :], raw["Wo"][:, k, :], start=k == 0, stop=k == KB - 1)
            last.then_inc(wo_row, 1)
            pe.wait_ge(heads_sb, 2)
            for k in range(KB):
                for hd in range(H):
                    last = pe.matmul(bank[5][:, k * HS + hd * SE:k * HS + (hd + 1) * SE], EqT[:, hd, k * P:(k + 1) * P],
                                     khT[:, hd, :], start=True, stop=True)
            last.then_inc(folded, 1)
            for k in range(KB):
                for b in range(KB):
                    last = pe.matmul(bank[6][:, k * SS:(k + 1) * SS], SinT[:, b, k * P:(k + 1) * P], knT[:, b, :],
                                     start=b == 0, stop=b == KB - 1)
            last.then_inc(folded, 1)
            pe.wait_ge(loads["Eo"], 16)
            for hd in range(H):
                last = pe.matmul(bank[7][:, :], vhT[:, hd, :], raw["Eo"][:, hd, :], start=hd == 0, stop=hd == H - 1)
            last.then_inc(folded, 1)

        @block.vector
        def _(dve):
            dve.memset(r["sign"][0:M, :], 1.0).then_inc(signed, 1)
            dve.memset(r["sign"][M:P, :], -1.0).then_inc(signed, 1)
            dve.wait_ge(small_T, 1)
            dve.tensor_copy(esT[:, :, :].rearrange("p k n -> p (k n)"), bank[4][:, 0:KB * SE]).then_inc(small_sb, 1)
            dve.wait_ge(small_T, 2)
            dve.tensor_copy(knT[:, :, :].rearrange("p k n -> p (k n)"), bank[5][:, 0:KB * SS]).then_inc(small_sb, 1)
            dve.wait_ge(loads["ln"], 32)
            dve.tensor_copy(lnb_w[:, :, :], lnb[:, :].unsqueeze(2).to_broadcast([P, KB, P])).then_inc(lnb_sb, 1)
            dve.wait_ge(zeroed, 5)
            dve.wait_ge(heads, 2)
            dve.wait_ge(heads_sb, 1)
            for hd in range(H):
                last = dve.tensor_copy(vhT[:, hd, hd * SE:(hd + 1) * SE], bank[5][:, hd * SE:(hd + 1) * SE])
            last.then_inc(heads_sb, 1)
            dve.wait_ge(wo_row, 1)
            dve.tensor_copy(r["bias_wo"][:, :], bank[0][:, :]).then_inc(wo_row_sb, 1)
            for k in range(KB):
                dve.tensor_scalar(raw["Wo"][:, k, :], raw["Wo"][:, k, :], lng[:, k:k + 1], None, ALU.mult).then_inc(wo_g, 1)
            dve.wait_ge(loads["kn"], 32)
            dve.tensor_copy(know_hl[0:SS, :], raw_kn[0:SS, :]).then_inc(kn_split, 1)
            dve.tensor_copy(kn_hi[SS:P, :], raw_kn[SS:P, :]).then_inc(kn_split, 1)
            dve.wait_ge(kn_split, 2)
            dve.tensor_tensor(know_hl[SS:P, :], raw_kn[SS:P, :], kn_hi[SS:P, :].bitcast(F32), ALU.subtract).then_inc(kn_split, 1)
            for n, (_, _, _, full, hi_t, lo_t) in enumerate(SPLITS):
                dve.wait_ge(hi, n + 1)
                dve.tensor_tensor(lo_t[:], full[:], hi_t[:].bitcast(F32), ALU.subtract).then_inc(lo, 1)
            dve.wait_ge(lo, len(SPLITS))
            dve.wait_ge(signed, 2)


def pass_b(nc, e):
    (bank, ident, half, blocks, split3) = (e[n] for n in ("bank", "ident", "half", "blocks", "split3"))
    NSEQ, D, KB, NE, GPS = (e[n] for n in ("NSEQ", "D", "KB", "NE", "GPS"))
    h_mid, out_g = e["h_mid"], e["out_g"]
    NS = e["sw1"].shape[1] // P
    NC = NS + NE
    KC = 32
    R1 = 16
    NBUF = 4

    with nc.cleanup_on_exit(), ExitStack() as ctx:
        def sb(name, shape, dt=F32):
            return ctx.enter_context(nc.sbuf_tensor(name, shape, dt))

        up_h, up_l = sb("up_h", [P, NC, KB, P], F32R), sb("up_l", [P, NC, KB, P], F32R)
        dn_h, dn_l = sb("dn_h", [P, NC, D], F32R), sb("dn_l", [P, NC, D], F32R)
        gw_h, gw_l = sb("gw_h", [P, KB, P], F32R), sb("gw_l", [P, KB, P], F32R)
        pick = sb("pick", [KC, NE, P], F32R)
        b2_h, b2_l = sb("b2_h", [KC, D], F32R), sb("b2_l", [KC, D], F32R)
        b_up = sb("b_up", [P, NC])
        before = sb("before", [P, NE, NE])
        ctok = sb("ctok", [P, T, KC], F32R)

        prep_b(nc, e, locals())

        h = [sb(f"hb{u}", [P, T, D]) for u in range(2)]
        xn = sb("xnb", [P, 2, D])
        xT_h, xT_l = sb("xTb_h", [P, KB, GT], F32R), sb("xTb_l", [P, KB, GT], F32R)
        act_b = sb("act_b", [P, 2, GT])
        hid_h, hid_l = sb("hid_h", [P, NBUF, GT], F32R), sb("hid_l", [P, NBUF, GT], F32R)
        cT = sb("cT", [KC, GT], F32R)
        glT = sb("glT", [NE, GT])
        s, c8 = sb("s", [P, T, NE]), sb("c8", [P, T, NE])
        gt, eq = sb("gt", [P, T, NE, NE]), sb("eq", [P, T, NE, NE])
        rank = sb("rank", [P, T, NE])
        smax, ssum, csum = sb("smax", [P, T]), sb("ssum", [P, T]), sb("csum", [P, T])
        bn6, mv, var_e = sb("bn6b", [P, T, 6]), sb("mvb", [P, T, 2]), sb("var_eb", [P, T])
        rstd, nmr = sb("rstdb", [P, T]), sb("nmrb", [P, T])

        BY_PE = dict(xT_ps=T, gl_ps=1, lg_ps=1, cT_ps=1, up_ps=NC, c_ps=NE, down=NC)
        BY_ACT = dict(xT_hi=T, glT=1, s_exp=1, cT_sb=1, relu=NC, hid_hi=NC)
        BY_DVE = dict(ln_bn=T, ln_stats=T, ln_bias=1, xT_lo=T, s_max=1, s_sub=1, s_sum=1, s_rec=1, s_done=1, gt=1, eq=1,
                      eq_before=1, beaten=1, rank=1, top=1, c_sum=1, c_eps=1, c_rec=1, c_done=1, c_hi=1, c_lo=1,
                      weighted=NE, hid_lo=NC, h_out=T)
        BY_POOL = dict(ln_var=1, ln_rstd=1, xn_rows=T)
        BY_DMA = {**{f"h_in{t}": 1 for t in range(T)}, **{f"h_stored{t}": 1 for t in range(T)}}
        per = {**BY_PE, **BY_ACT, **BY_DVE, **BY_POOL, **BY_DMA}
        sem = {name: nc.alloc_semaphore("B_" + name) for name in per}

        def at(name, g, k=0):
            step = 16 if name in BY_DMA else 1
            return (g + 1) * (per[name] * step) + (k + 1) * step

        def wait(eng, name, g, k=0):
            eng.wait_ge(sem[name], at(name, g, k))

        unread = nc.alloc_semaphore("B_unread")

        def waits_end(eng):
            eng.sem_inc(unread, 1)

        def credit(eng, names, step=1):
            for name in names:
                eng.sem_inc(sem[name], per[name] * step)

        USES = [("gl", "glT", 0), ("up0", "relu", 0), ("lg", "s_sub", 0), ("up1", "relu", 1), ("up2", "relu", 2),
                ("up3", "relu", 3), ("cT", "cT_sb", 0)]
        for j in range(NS, NC):
            USES += [(f"up{j}", "relu", j), (f"c{j - NS}", "weighted", j - NS)]
        USES += [(f"xT{t}", "xT_lo", t) for t in range(T)]
        RING = 4
        assert NS == RING
        place = {use[0]: i for i, use in enumerate(USES)}

        def ps(use):
            return bank[place[use] % RING]

        def bank_free(pe, use, g):
            i, slot = place[use] - RING, g
            if i < 0:
                slot = g - 1
                i = max(j for j in range(len(USES)) if j % RING == place[use] % RING)
            before_it, signal, k = USES[i]
            wait(pe, signal, slot + 1 if before_it.startswith("xT") else slot, k)

        block = ctx.enter_context(nc.Block())

        def loop(eng, body):
            with eng.Fori(0, NSEQ - 1) as i:
                for u in range(GPS):
                    body(i * GPS + u, u, False)
            for u in range(GPS):
                body((NSEQ - 1) * GPS + u, u, u == GPS - 1)

        @block.sync
        def _(sp):
            credit(sp, BY_DMA, 16)

            def load(g, u):
                for t in range(T):
                    wait(sp, f"h_stored{t}", g - 2)
                    wait(sp, f"h_in{t}", g - 1)
                    sp.dma_start(h[u][:, t, :], h_mid[g, t]).then_inc(sem[f"h_in{t}"], 16)
            for t in range(T):
                sp.dma_start(h[0][:, t, :], h_mid[0, t]).then_inc(sem[f"h_in{t}"], 16)

            def body(g, u, last):
                if not last:
                    load(g + 1, (u + 1) % GPS)
                for t in range(T):
                    wait(sp, "h_out", g, t)
                    sp.dma_start(out_g[g, t], h[u][:, t, :]).then_inc(sem[f"h_stored{t}"], 16)
            loop(sp, body)
            for t in range(T):
                wait(sp, f"h_stored{t}", NSEQ * GPS - 1)

        @block.gpsimd
        def _(pool):
            credit(pool, BY_POOL)

            def ln(g, u):
                wait(pool, "ln_stats", g, T - 1)
                wait(pool, "ln_rstd", g - 1)
                waits_end(pool)
                pool.tensor_scalar(var_e[:, :], mv[:, :, 1], LN_EPS, None, ALU.add).then_inc(sem["ln_var"], 1)
                wait(pool, "ln_var", g)
                wait(pool, "xn_rows", g - 1, T - 1)
                pool.tensor_tensor(rstd[:, :], var_e[:, :], half[:, :], ALU.pow).then_inc(sem["ln_rstd"], 1)
                wait(pool, "ln_bias", g)
                for t in range(T):
                    if t >= 2:
                        wait(pool, "xT_ps", g, t - 2)
                    else:
                        wait(pool, "xT_ps", g - 1, t + 2)
                    waits_end(pool)
                    pool.tensor_scalar(xn[:, t % 2, :], h[u][:, t, :], rstd[:, t:t + 1], nmr[:, t:t + 1],
                                       ALU.mult, ALU.add).then_inc(sem["xn_rows"], 1)
            ln(0, 0)

            def body(g, u, last):
                if not last:
                    ln(g + 1, (u + 1) % GPS)
            loop(pool, body)

        @block.scalar
        def _(act):
            credit(act, BY_ACT)

            def xT_hi(g):
                for t in range(T):
                    wait(act, "xT_ps", g, t)
                    if t == 0:
                        wait(act, "up_ps", g - 1, NC - 1)
                    act.activation(xT_h[:, :, t * P:(t + 1) * P], ps(f"xT{t}")[:, :].rearrange("p (k n) -> p k n", k=KB),
                                   ACT.Copy).then_inc(sem["xT_hi"], 1)
            xT_hi(0)

            def hid_hi(g, j):
                if j < NS:
                    wait(act, "relu", g, j)
                else:
                    wait(act, "weighted", g, j - NS)
                if j >= NBUF:
                    wait(act, "down", g, j - NBUF)
                else:
                    wait(act, "down", g - 1, NC - NBUF + j)
                act.activation(hid_h[:, j % NBUF, :], act_b[:, j % 2, :], ACT.Copy).then_inc(sem["hid_hi"], 1)

            def body(g, u, last):
                wait(act, "gl_ps", g)
                wait(act, "lg_ps", g - 1)
                act.activation(glT[:, :], ps("gl")[0:NE, :], ACT.Copy).then_inc(sem["glT"], 1)
                for j in range(NC):
                    wait(act, "up_ps", g, j)
                    if j >= 2:
                        wait(act, "hid_lo", g, j - 2)
                    else:
                        wait(act, "hid_lo", g - 1, NC - 2 + j)
                    act.activation(act_b[:, j % 2, :], ps(f"up{j}")[:, :], ACT.Relu, bias=b_up[:, j:j + 1])\
                       .then_inc(sem["relu"], 1)
                    if j == 1:
                        wait(act, "s_sub", g)
                        act.activation(s[:, :, :], s[:, :, :], ACT.Exp).then_inc(sem["s_exp"], 1)
                    if j == NS - 1:
                        wait(act, "cT_ps", g)
                        wait(act, "c_ps", g - 1, NE - 1)
                        act.activation(cT[:, :], ps("cT")[0:KC, :], ACT.Copy).then_inc(sem["cT_sb"], 1)
                    hid_hi(g, j)
                if not last:
                    xT_hi(g + 1)
            loop(act, body)

        @block.tensor
        def _(pe):
            credit(pe, BY_PE)

            def xT(g, slot):
                for t in range(T):
                    wait(pe, "xn_rows", g, t)
                    bank_free(pe, f"xT{t}", slot)
                    for k in range(KB):
                        last = pe.transpose(ps(f"xT{t}")[:, k * P:(k + 1) * P], xn[:, t % 2, k * P:(k + 1) * P],
                                            ident[:, :])
                    last.then_inc(sem["xT_ps"], 1)

            def by_feature(g, use, signal, wh, wl):
                bank_free(pe, use, g)
                for k in range(KB):
                    last = split3(pe, ps(use)[:, :], wh(k), wl(k), xT_h[:, k, :], xT_l[:, k, :], k == 0, k == KB - 1)
                last.then_inc(sem[signal], 1)

            def down(g, j):
                wait(pe, "hid_lo", g, j)
                for t in range(T):
                    if j == 0:
                        wait(pe, "h_out", g - 1, t)
                    cols = slice(t * P, (t + 1) * P)
                    last = split3(pe, bank[RING + t][:, :], hid_h[:, j % NBUF, cols], hid_l[:, j % NBUF, cols],
                                  dn_h[:, j, :], dn_l[:, j, :], j == 0, j == NC - 1)
                last.then_inc(sem["down"], 1)

            xT(0, -1)

            def body(g, u, last_group):
                wait(pe, "xT_lo", g, T - 1)
                by_feature(g, "gl", "gl_ps", lambda k: gw_h[:, k, :], lambda k: gw_l[:, k, :])
                for j in range(NC):
                    by_feature(g, f"up{j}", "up_ps", lambda k: up_h[:, j, k, :], lambda k: up_l[:, j, k, :])
                    if j == 0:
                        wait(pe, "glT", g)
                        bank_free(pe, "lg", g)
                        waits_end(pe)
                        for t in range(T):
                            last = pe.transpose(ps("lg")[:, t * NE:(t + 1) * NE], glT[:, t * P:(t + 1) * P],
                                                ident[0:NE, 0:NE])
                        last.then_inc(sem["lg_ps"], 1)
                    if j >= NS:
                        if j == NS:
                            wait(pe, "cT_sb", g)
                        bank_free(pe, f"c{j - NS}", g)
                        pe.matmul(ps(f"c{j - NS}")[:, :], pick[:, j - NS, :], cT[:, :], start=True, stop=True)\
                          .then_inc(sem["c_ps"], 1)
                    if j == NC - 1 and not last_group:
                        xT(g + 1, g)
                    if j >= 2:
                        down(g, j - 2)
                    if j == NS - 1:
                        wait(pe, "c_lo", g)
                        bank_free(pe, "cT", g)
                        for t in range(T):
                            last = pe.transpose(ps("cT")[0:KC, t * P:(t + 1) * P], ctok[:, t, :].bitcast(F32), ident[:, :])
                        last.then_inc(sem["cT_ps"], 1)
                    if j == NC - 1:
                        for t in range(T):
                            cols = slice(t * P, (t + 1) * P)
                            pe.matmul(bank[RING + t][:, :], cT[:, cols], b2_h[:, :], start=False, stop=False)
                            pe.matmul(bank[RING + t][:, :], cT[:, cols], b2_l[:, :], start=False, stop=False)
                down(g, NC - 2)
                down(g, NC - 1)
            loop(pe, body)

        @block.vector
        def _(dve):
            credit(dve, BY_DVE)

            def done(ins, name):
                ins.then_inc(sem[name], 1)

            def ln_stats(g, u):
                for t in range(T):
                    wait(dve, f"h_in{t}", g)
                    if t == 0:
                        wait(dve, "ln_var", g - 1)
                        wait(dve, "ln_bias", g - 1)
                    done(dve.bn_stats(bn6[:, t, :], h[u][:, t, :]), "ln_bn")
                for t in range(T):
                    wait(dve, "ln_bn", g, t)
                    waits_end(dve)
                    done(dve.bn_aggr(mv[:, t, :], bn6[:, t, :]), "ln_stats")

            def ln_bias(g):
                wait(dve, "ln_rstd", g)
                wait(dve, "xn_rows", g - 1, T - 1)
                done(dve.scalar_tensor_tensor(nmr[:, :], mv[:, :, 0], -1.0, rstd[:, :], ALU.mult, ALU.mult), "ln_bias")

            def xT_lo(g):
                for t in range(T):
                    wait(dve, "xT_hi", g, t)
                    cols = slice(t * P, (t + 1) * P)
                    done(dve.tensor_tensor(xT_l[:, :, cols], ps(f"xT{t}")[:, :].rearrange("p (k n) -> p k n", k=KB),
                                           xT_h[:, :, cols].bitcast(F32), ALU.subtract), "xT_lo")

            def hid_lo(g, j):
                wait(dve, "hid_hi", g, j)
                done(dve.tensor_tensor(hid_l[:, j % NBUF, :], act_b[:, j % 2, :], hid_h[:, j % NBUF, :].bitcast(F32),
                                       ALU.subtract), "hid_lo")

            def over_experts(a):
                return a[:, :].unsqueeze(2).to_broadcast([P, T, NE])

            def route(g):
                wait(dve, "lg_ps", g)
                lg = ps("lg")[:, 0:T * NE].rearrange("p (t n) -> p t n", t=T)
                done(dve.tensor_reduce(smax[:, :], lg, AX.X, ALU.max), "s_max")
                wait(dve, "s_max", g)
                done(dve.tensor_tensor(s[:, :, :], lg, over_experts(smax), ALU.subtract), "s_sub")

            def top2(g):
                wait(dve, "s_exp", g)
                done(dve.tensor_reduce(ssum[:, :], s[:, :, :], AX.X, ALU.add), "s_sum")
                wait(dve, "s_sum", g)
                done(dve.reciprocal(ssum[:, :], ssum[:, :]), "s_rec")
                wait(dve, "s_rec", g)
                done(dve.tensor_tensor(s[:, :, :], s[:, :, :], over_experts(ssum), ALU.mult), "s_done")
                wait(dve, "s_done", g)
                other = s[:, :, :].unsqueeze(2).to_broadcast([P, T, NE, NE])
                own = s[:, :, :].unsqueeze(3).to_broadcast([P, T, NE, NE])
                done(dve.tensor_tensor(gt[:, :, :, :], other, own, ALU.is_gt), "gt")
                done(dve.tensor_tensor(eq[:, :, :, :], other, own, ALU.is_equal), "eq")
                wait(dve, "eq", g)
                done(dve.tensor_tensor(eq[:, :, :, :], eq[:, :, :, :],
                                       before[:, :, :].unsqueeze(1).to_broadcast([P, T, NE, NE]), ALU.mult), "eq_before")
                wait(dve, "gt", g)
                wait(dve, "eq_before", g)
                done(dve.tensor_tensor(gt[:, :, :, :], gt[:, :, :, :], eq[:, :, :, :], ALU.add), "beaten")
                wait(dve, "beaten", g)
                done(dve.tensor_reduce(rank[:, :, :], gt[:, :, :, :], AX.X, ALU.add), "rank")
                wait(dve, "rank", g)
                done(dve.scalar_tensor_tensor(c8[:, :, :], rank[:, :, :], 1.5, s[:, :, :], ALU.is_lt, ALU.mult), "top")
                wait(dve, "top", g)
                done(dve.tensor_reduce(csum[:, :], c8[:, :, :], AX.X, ALU.add), "c_sum")
                wait(dve, "c_sum", g)
                done(dve.tensor_scalar(csum[:, :], csum[:, :], TOPK_EPS, None, ALU.add), "c_eps")
                wait(dve, "c_eps", g)
                done(dve.reciprocal(csum[:, :], csum[:, :]), "c_rec")
                wait(dve, "c_rec", g)
                done(dve.tensor_tensor(c8[:, :, :], c8[:, :, :], over_experts(csum), ALU.mult), "c_done")
                wait(dve, "c_done", g)
                wait(dve, "cT_ps", g - 1)
                done(dve.tensor_copy(ctok[:, :, 0:NE], c8[:, :, :]), "c_hi")
                wait(dve, "c_hi", g)
                done(dve.tensor_tensor(ctok[:, :, NE:2 * NE], c8[:, :, :], ctok[:, :, 0:NE].bitcast(F32), ALU.subtract), "c_lo")

            ln_stats(0, 0)
            ln_bias(0)
            xT_lo(0)

            def body(g, u, last):
                for j in range(NC):
                    if j >= NS:
                        wait(dve, "c_ps", g, j - NS)
                        wait(dve, "relu", g, j)
                        done(dve.tensor_tensor(act_b[:, j % 2, :], act_b[:, j % 2, :], ps(f"c{j - NS}")[:, :], ALU.mult),
                             "weighted")
                    if j == 1:
                        route(g)
                    hid_lo(g, j)
                    if j == 1:
                        top2(g)
                    if j == NS and not last:
                        ln_stats(g + 1, (u + 1) % GPS)
                    if j == NS + 1 and not last:
                        ln_bias(g + 1)
                if not last:
                    xT_lo(g + 1)
                for t in range(T):
                    wait(dve, "down", g, NC - 1)
                    done(dve.tensor_tensor(h[u][:, t, :], bank[RING + t][:, :], h[u][:, t, :], ALU.add), "h_out")
            loop(dve, body)


def prep_b(nc, e, r):
    bank, ident, blocks = e["bank"], e["ident"], e["blocks"]
    KB, NE, D, NS, NC, KC, R1 = (r[n] for n in ("KB", "NE", "D", "NS", "NC", "KC", "R1"))
    with nc.cleanup_on_exit(), ExitStack() as ctx:
        def sb(name, shape, dt=F32):
            return ctx.enter_context(nc.sbuf_tensor(name, shape, dt))

        def new(name):
            return nc.alloc_semaphore("PB_" + name)

        raw_up, raw_dn = sb("raw_up", [P, NC, KB, P]), sb("raw_dn", [P, NC, D])
        raw_gw, gw = sb("raw_gw", [NE, D]), sb("gw", [P, KB, P])
        raw_b2, raw_pick = sb("raw_b2", [KC, D]), sb("raw_pick", [KC, NE, P])
        up_in, dn_in = [new(f"up_in{j}") for j in range(NC)], [new(f"dn_in{j}") for j in range(2)]
        gw_in, b2_in, b_in = new("gw_in"), new("b2_in"), new("b_in")
        zeroed, b2_zero, picks, before_ok, ones_in = new("zeroed"), new("b2_zero"), new("picks"), new("before_ok"), new("ones_in")
        gw_T, gw_sb, hi, lo = new("gw_T"), new("gw_sb"), new("hi"), new("lo")

        SPLITS = [(gw_sb, 1, gw[:], r["gw_h"][:], r["gw_l"][:])]
        for j in range(NC):
            SPLITS.append((up_in[j], 16, raw_up[:, j], r["up_h"][:, j], r["up_l"][:, j]))
        SPLITS.append((b2_in, 48, raw_b2[:], r["b2_h"][:], r["b2_l"][:]))
        for j in range(NC):
            SPLITS.append((dn_in[j >= NS], 16, raw_dn[:, j], r["dn_h"][:, j], r["dn_l"][:, j]))

        block = ctx.enter_context(nc.Block())

        @block.sync
        def _(sp):
            sp.dma_start(raw_gw[:, :], e["gate_w"]).then_inc(gw_in, 16)
            for j in range(0, NC, 2):
                w = e["sw1"][:, j * P:(j + 1) * P] if j < NS else e["w1"][j - NS]
                sp.dma_start(raw_up[:, j], blocks(w)).then_inc(up_in[j], 16)
            sp.dma_start(raw_dn[:, 0:NS, :], e["sw2"].rearrange("(j p) n -> p j n", p=P)).then_inc(dn_in[0], 16)
            sp.wait_ge(b2_zero, 1)
            sp.dma_start(raw_b2[0:NE, :], e["b2"]).then_inc(b2_in, 16)
            sp.dma_start(raw_b2[NE:2 * NE, :], e["b2"]).then_inc(b2_in, 16)
            sp.dma_start(raw_b2[R1:R1 + 1, :], e["sb2"].rearrange("(a n) -> a n", a=1)).then_inc(b2_in, 16)

        @block.scalar
        def _(act):
            for j in range(1, NC, 2):
                w = e["sw1"][:, j * P:(j + 1) * P] if j < NS else e["w1"][j - NS]
                act.dma_start(raw_up[:, j], blocks(w)).then_inc(up_in[j], 16)
            act.dma_start(raw_dn[:, NS:NC, :], e["w2"].rearrange("j p n -> p j n")).then_inc(dn_in[1], 16)
            for ready, value, full, hi_t, _ in SPLITS:
                act.wait_ge(ready, value)
                act.activation(hi_t, full, ACT.Copy).then_inc(hi, 1)

        @block.gpsimd
        def _(pool):
            pool.memset(raw_b2[:, :], 0.0).then_inc(b2_zero, 1)
            pool.memset(raw_pick[:], 0.0).then_inc(picks, 1)
            pool.memset(r["before"][:], 1.0).then_inc(before_ok, 1)
            pool.memset(gw[:], 0.0).then_inc(zeroed, 1)
            for z in range(2):
                pool.wait_ge(picks, z + 1)
                pool.affine_select(out=raw_pick[:], in_=raw_pick[:], compare_op=ALU.not_equal, fill=1.0, base=-z * NE,
                                   pattern=[[-1, NE], [0, P]], channel_multiplier=1).then_inc(picks, 1)
            pool.wait_ge(before_ok, 1)
            pool.affine_select(out=r["before"][:], in_=r["before"][:], compare_op=ALU.is_gt, fill=0.0, base=0,
                               pattern=[[1, NE], [-1, NE]], channel_multiplier=0).then_inc(before_ok, 1)
            pool.dma_start(r["b_up"][:, 0:NS], e["sb1"].rearrange("(j p) -> p j", p=P), allow_slow_non_contiguous=True)\
                .then_inc(b_in, 16)
            pool.dma_start(r["b_up"][:, NS:NC], e["b1"].rearrange("j p -> p j"), allow_slow_non_contiguous=True)\
                .then_inc(b_in, 16)
            pool.wait_ge(b_in, 32)
            pool.wait_ge(before_ok, 2)

        @block.tensor
        def _(pe):
            pe.wait_ge(gw_in, 16)
            for k in range(KB):
                last = pe.transpose(bank[0][:, k * NE:(k + 1) * NE], raw_gw[:, k * P:(k + 1) * P], ident[0:NE, 0:NE])
            last.then_inc(gw_T, 1)

        @block.vector
        def _(dve):
            dve.memset(r["ctok"][:].bitcast(F32), 0.0).then_inc(ones_in, 1)
            dve.wait_ge(ones_in, 1)
            dve.memset(r["ctok"][:, :, R1:R1 + 1].bitcast(F32), 1.0).then_inc(ones_in, 1)
            dve.wait_ge(zeroed, 1)
            dve.wait_ge(gw_T, 1)
            dve.tensor_copy(gw[:, :, 0:NE], bank[0][:, 0:KB * NE].rearrange("p (k n) -> p k n", k=KB)).then_inc(gw_sb, 1)
            dve.wait_ge(picks, 3)
            dve.tensor_copy(r["pick"][:], raw_pick[:]).then_inc(ones_in, 1)
            for n, (_, _, full, hi_t, lo_t) in enumerate(SPLITS):
                dve.wait_ge(hi, n + 1)
                dve.tensor_tensor(lo_t, full, hi_t.bitcast(F32), ALU.subtract).then_inc(lo, 1)
            dve.wait_ge(lo, len(SPLITS))
            dve.wait_ge(ones_in, 3)


def kernel(x, L0_tok_embed_matrix, **weights):
    import numpy as np
    import concourse.bacc as bacc
    from concourse import mybir as _mybir
    from concourse.bass_utils import run_bass_kernel_spmd

    x = np.asarray(x)
    batch, length = x.shape
    arrays = {"x": np.ascontiguousarray(x.reshape(batch, length // P, P).transpose(0, 2, 1)),
              "emb": np.ascontiguousarray(L0_tok_embed_matrix)}
    for name, value in weights.items():
        arrays[name.split("_", 2)[2]] = np.ascontiguousarray(value)
    nc = bacc.Bacc("TRN2", target_bir_lowering=False, num_devices=1)
    args = {n: nc.dram_tensor("in_" + n, a.shape, _mybir.dt.from_np(a.dtype), kind="ExternalInput").ap()
            for n, a in arrays.items()}
    width = arrays["emb"].shape[1]
    out = nc.dram_tensor("out", (batch, length, width), _mybir.dt.from_np(np.dtype("float32")), kind="ExternalOutput").ap()
    lm_tower(nc, args.pop("x"), args.pop("emb"), **args, out=out)
    r = run_bass_kernel_spmd(nc, [{"in_" + n: a for n, a in arrays.items()}], core_ids=[0])
    return r.results[0]["out"]
```

```python
from contextlib import ExitStack

import concourse.bass as bass
from concourse import mybir

F32 = mybir.dt.float32
F32R = mybir.dt.float32r
I32 = mybir.dt.int32
ALU = mybir.AluOpType
ACT = mybir.ActivationFunctionType
AX = mybir.AxisListType

P = 128
T = 4
GT = T * P
LN_EPS = 1e-5
DEN_EPS = 1e-6
FORGET_MIN = 1e-6
LOG_CLIP = 20.0
F_CLIP = -30.0
TOPK_EPS = 1e-20


def lm_tower(nc, x_idx, emb, Wq, Wk, Wv, Wf, bf, Wo, ln_g, ln_b, eslots, Eq, Ek, Ev, Eo, know, Sin, Sg_w, Sg_b,
             So, C1w, C1b, C2w, C2b, gate_w, w1, b1, w2, b2, sw1, sb1, sw2, sb2, out):
    NSEQ, _, TILES = x_idx.shape
    D = emb.shape[1]
    KB = D // P
    M = Wq.shape[1]
    SE, SS = eslots.shape[1], know.shape[1]
    HD = P
    H = D // HD
    BOT = C1w.shape[1]
    NE, _, DF = w1.shape
    GPS = TILES // T
    assert GPS == 2 and M == 64 and H * SE == P and BOT == P and DF == P and D == GT
    WES = H * SE + SS
    Q_SCALE = float(M) ** -0.5

    h_mid = nc.dram_tensor("h_mid", (NSEQ * GPS, T, P, D), F32, kind="Internal").ap()
    out_g = out.rearrange("b (u t p) d -> (b u) t p d", t=T, p=P)

    def blocks(w):
        return w.rearrange("(k p) n -> p k n", p=P)

    def split3(pe, o, wh, wl, mh, ml, start, stop):
        pe.matmul(o, wh, mh, start=start, stop=False)
        pe.matmul(o, wh, ml, start=False, stop=False)
        return pe.matmul(o, wl, mh, start=False, stop=stop)

    with ExitStack() as whole:
        bank = [whole.enter_context(nc.psum_tensor(f"bank{b}", [P, GT], F32)) for b in range(8)]
        ident = whole.enter_context(nc.sbuf_tensor("ident", [P, P], F32))
        half = whole.enter_context(nc.sbuf_tensor("half", [P, T], F32))
        pass_a(nc, locals())
        pass_b(nc, locals())


def pass_a(nc, e):
    (bank, ident, half, blocks, split3) = (e[n] for n in ("bank", "ident", "half", "blocks", "split3"))
    (NSEQ, TILES, D, KB, M, SE, SS, H, GPS, WES, Q_SCALE) = (
        e[n] for n in ("NSEQ", "TILES", "D", "KB", "M", "SE", "SS", "H", "GPS", "WES", "Q_SCALE"))
    x_idx, emb, h_mid = e["x_idx"], e["emb"], e["h_mid"]
    HS = H * SE

    with nc.cleanup_on_exit(), ExitStack() as ctx:
        def sb(name, shape, dt=F32):
            return ctx.enter_context(nc.sbuf_tensor(name, shape, dt))

        SPLIT = (("qkf", (KB, 4 * M)),
                 ("c1", (KB, P)), ("se", (KB, HS)),
                 ("v", (KB, D)), ("sg", (KB, D)), ("so", (KB, D)), ("wo", (KB, D)), ("ve", (D,)))
        w_hi = {n: sb(f"w{n}_h", [P, *cols], F32R) for n, cols in SPLIT}
        with ExitStack() as arrival:
            full = {n: arrival.enter_context(nc.sbuf_tensor(f"w{n}_full", [P, *cols], F32)) for n, cols in SPLIT}
        w_lo = {n: sb(f"w{n}_l", [P, *cols], F32R) for n, cols in SPLIT}
        know_hl = sb("know_hl", [P, D], F32R)
        bias_wo = sb("bias_wo", [P, D])
        c2w = sb("c2w", [P, 3])
        c2b = sb("c2b", [P, 3])
        c1b = sb("c1b", [P, 1])
        sgb = sb("sgb", [P, KB])
        bff = sb("bff", [P, 1])
        sign = sb("sign", [P, 1])
        ones = sb("ones", [P, 1])
        causal = sb("causal", [P, P])

        h = [sb(f"h{u}", [P, T, D]) for u in range(2)]
        idx = sb("idx", [P, TILES], I32)
        xn = sb("xn", [P, T, D])
        xT_h, xT_l = sb("xT_h", [P, KB, GT], F32R), sb("xT_l", [P, KB, GT], F32R)
        bn6, mv, var_e = sb("bn6", [P, T, 6]), sb("mv", [P, T, 2]), sb("var_e", [P, T])
        rstd, nmr = sb("rstd", [P, T]), sb("nmr", [P, T])

        BY_PE = dict(xT_ps=T, c1_ps=1, fs_ps=1, qk_ps=1, e_ps=1, eT_ps=1, kS_ps=1, v_ps=T, kT_ps=1, a_ps=1, small_ps=1,
                     state_ps=T, num_ps=T, nT_ps=T, aT_ps=1, sT_ps=1, ret_ps=KB, gate_ps=KB, so_ps=T, out_ps=T)
        BY_ACT = dict(xT_hi=T, c1_sig=1, kS_sb=1, e_sb=1, f_exp=1, qk_exp=1, ln_u=1, decay=1, es_exp=2, q_hi=1, k_hi=2,
                      v_hi=T, w_exp=1, kT_sb=1, a_hi=1, s_hi=T, n_rows=T, nT_hi=T, aT_hi=1, sT_hi=1, gate=KB,
                      mix_hi=KB)
        BY_DVE = dict(ln_bn=T, ln_stats=T, ln_bias=1, xT_lo=T, silu=1, f_clip=1, qk_min=1, u=1, qk_elu=1, lsum_raw=1, l_clip=2, l_carry=1, q_dup=2,
                      k_dec=1, z_sum=1, z_carry=1, qz=1, q_lo=1, k_lo=1, es_max=2, es_sub=2, es_sum=2, es_rec=1, lg_add=1,
                      den_add=1, den_rec=1, den_sq=1, lg_max=1, lg_sub=1, w_sum=1, w_rec=1, w_done=1, rE_w=1, rd_w=1,
                      v_lo=T, a_mask=1, a_lo=1, s_lo=T, n_bn=T, n_stats=T, n_var=T, n_scale=T, n_bias=T, nT_lo=T, aT_lo=1,
                      sT_lo=1, xg=KB, mix_mul=KB, mix=KB, mix_lo=KB, h_bias=T, h_so=T, h_out=T)
        BY_POOL = dict(ln_var=1, ln_rstd=1, xn_rows=T, n_rstd=T, probs=3, xf=KB)
        BY_DMA = {**{f"h_in{t}": 1 for t in range(T)}, **{f"h_stored{t}": 1 for t in range(T)}}
        per = {**BY_PE, **BY_ACT, **BY_DVE, **BY_POOL, **BY_DMA}
        sem = {name: nc.alloc_semaphore("A_" + name) for name in per}
        idx_in = nc.alloc_semaphore("A_idx_in")

        def at(name, g, k=0):
            step = 16 if name in BY_DMA else 1
            before = g if name.startswith("h_in") else g + 1
            return before * (per[name] * step) + (k + 1) * step

        def wait(eng, name, g, k=0):
            eng.wait_ge(sem[name], at(name, g, k))

        unread = nc.alloc_semaphore("A_unread")

        def waits_end(eng):
            eng.sem_inc(unread, 1)

        def credit(eng, names, step=1):
            for name in names:
                eng.sem_inc(sem[name], per[name] * step)

        USES = [("fs", "f_clip", 0), ("c1", "silu", 0), ("qk", "qk_elu", 0), ("e", "e_sb", 0), ("v0", "v_lo", 0),
                ("eT", "es_sub", 1), ("kS", "den_add", 0), ("v1", "v_lo", 1), ("kT", "kT_sb", 0), ("a", "a_mask", 0),
                ("gate0", "gate", 0), ("num0", "n_rows", 0), ("v2", "v_lo", 2), ("num1", "n_rows", 1),
                ("v3", "v_lo", 3), ("num2", "n_rows", 2), ("nT0", "nT_lo", 0), ("gate1", "gate", 1), ("nT1", "nT_lo", 1),
                ("num3", "n_rows", 3), ("sT", "sT_lo", 0), ("aT", "aT_lo", 0), ("gate2", "gate", 2),
                ("ret0", "mix_mul", 0), ("ret1", "mix_mul", 1), ("gate3", "gate", 3), ("ret2", "mix_mul", 2),
                ("ret3", "mix_mul", 3), ("out0", "h_out", 0), ("nT2", "nT_lo", 2), ("out1", "h_out", 1),
                ("nT3", "nT_lo", 3)]
        USES += [(f"so{t}", "h_so", t) for t in range(T)]
        USES += [(f"xT{t}", "xT_lo", t) for t in range(T)] + [("out2", "h_out", 2), ("out3", "h_out", 3)]
        RING = 7
        assert len(USES) % RING == 0
        place = {use[0]: i for i, use in enumerate(USES)}
        place["small"] = place["kS"]
        state = bank[RING]

        def ps(use):
            return bank[place[use] % RING]

        def bank_free(pe, use, g):
            i = place[use] - RING
            before, signal, k = USES[i]
            slot = g - 1 if i < 0 else g
            wait(pe, signal, slot + 1 if before.startswith("xT") else slot, k)

        def flat(t):
            return t.rearrange("p a b -> p (a b)")

        def done(ins, name):
            ins.then_inc(sem[name], 1)

        def gather(pool, g, u):
            for t in range(T):
                if not (isinstance(g, int) and g < GPS):
                    wait(pool, f"h_stored{t}", g - 2)
                    waits_end(pool)
                pool.indirect_dma_start(
                    out=h[u][:, t, :], out_offset=None, in_=emb[:, :],
                    in_offset=bass.IndirectOffsetOnAxis(ap=idx[:, u * T + t:u * T + t + 1], axis=0),
                ).then_inc(sem[f"h_in{t}"], 16)

        def ln_scale(pool, g):
            wait(pool, "ln_stats", g, T - 1)
            wait(pool, "ln_rstd", g - 1)
            waits_end(pool)
            pool.tensor_scalar(var_e[:, :], mv[:, :, 1], LN_EPS, None, ALU.add).then_inc(sem["ln_var"], 1)
            wait(pool, "ln_var", g)
            wait(pool, "xn_rows", g - 1, T - 1)
            pool.tensor_tensor(rstd[:, :], var_e[:, :], half[:, :], ALU.pow).then_inc(sem["ln_rstd"], 1)

        def ln_rows(pool, g, u, tiles):
            wait(pool, "ln_bias", g)
            for t in tiles:
                wait(pool, "xT_ps", g - 1, t)
                waits_end(pool)
                pool.tensor_scalar(xn[:, t, :], h[u][:, t, :], rstd[:, t:t + 1], nmr[:, t:t + 1],
                                   ALU.mult, ALU.add).then_inc(sem["xn_rows"], 1)

        def xT_hi(act, g):
            for t in range(T):
                wait(act, "xT_ps", g, t)
                if t == 0:
                    wait(act, "xf", g - 1, KB - 1)
                    wait(act, "gate_ps", g - 1, KB - 1)
                act.activation(xT_h[:, :, t * P:(t + 1) * P], ps(f"xT{t}")[:, :].rearrange("p (k n) -> p k n", k=KB),
                               ACT.Copy).then_inc(sem["xT_hi"], 1)

        def xT(pe, g, slot):
            for t in range(T):
                wait(pe, "xn_rows", g, t)
                bank_free(pe, f"xT{t}", slot)
                for k in range(KB):
                    last = pe.transpose(ps(f"xT{t}")[:, k * P:(k + 1) * P], xn[:, t, k * P:(k + 1) * P],
                                        ident[:, :])
                last.then_inc(sem["xT_ps"], 1)

        def ln_stats(dve, g, u, tiles):
            for t in tiles:
                wait(dve, f"h_in{t}", g)
                if t == 0:
                    wait(dve, "ln_var", g - 1)
                    wait(dve, "ln_bias", g - 1)
                done(dve.bn_stats(bn6[:, t, :], h[u][:, t, :]), "ln_bn")
            for t in tiles:
                wait(dve, "ln_bn", g, t)
                waits_end(dve)
                done(dve.bn_aggr(mv[:, t, :], bn6[:, t, :]), "ln_stats")

        def ln_bias(dve, g):
            wait(dve, "ln_rstd", g)
            wait(dve, "xn_rows", g - 1, T - 1)
            done(dve.scalar_tensor_tensor(nmr[:, :], mv[:, :, 0], -1.0, rstd[:, :], ALU.mult, ALU.mult), "ln_bias")

        def xT_lo(dve, g):
            for t in range(T):
                wait(dve, "xT_hi", g, t)
                cols = slice(t * P, (t + 1) * P)
                done(dve.tensor_tensor(xT_l[:, :, cols], ps(f"xT{t}")[:, :].rearrange("p (k n) -> p k n", k=KB),
                                       xT_h[:, :, cols].bitcast(F32), ALU.subtract), "xT_lo")

        prep_a(nc, e, locals())

        ef = sb("ef", [P, GT])
        dec = sb("dec", [P, GT])
        qk = sb("qk", [P, GT])
        mix1 = sb("mix1", [P, GT])
        am = sb("am", [P, GT])
        c1s = sb("c1s", [P, GT])
        gate_b, mix_b, xf_b = [ef, dec], [qk, mix1], [am, c1s]
        lraw = sb("lraw", [P, GT])
        carry = sb("carry", [P, 2])
        q2 = sb("q2", [P, GT])
        q2_h, q2_l = sb("q2_h", [P, GT], F32R), sb("q2_l", [P, GT], F32R)
        kf = sb("kf", [M, GT])
        kh = sb("kh", [M, GT], F32R)
        zc = sb("zc", [M, GT])
        k_hl = sb("k_hl", [P, GT], F32R)
        kT_hl = sb("kT_hl", [P, T, P], F32R)
        a_h, a_l = sb("a_h", [P, GT], F32R), sb("a_l", [P, GT], F32R)
        aT_h, aT_l = a_h, a_l
        sT_h, sT_l = q2_h, q2_l
        v_h, v_l = sb("v_h", [P, 2, D], F32R), sb("v_l", [P, 2, D], F32R)
        nT_h, nT_l = v_h, v_l
        s_h, s_l = sb("s_h", [P, D], F32R), sb("s_l", [P, D], F32R)
        n = sb("n", [P, 2, D])
        mixT_h, mixT_l = sb("mixT_h", [P, KB, GT], F32R), sb("mixT_l", [P, KB, GT], F32R)
        sx = sb("sx", [P, T, WES])
        pr = sb("pr", [P, T, 2 * P])
        mE, mS = sb("mE", [P, T, H]), sb("mS", [P, T])
        rs = sb("rs", [P, T, H + 1])
        nb6, nmv, nv = sb("nb6", [P, T, 6]), sb("nmv", [P, T, 2]), sb("nv", [P, T])
        nrs, nsc, nbi = sb("nrs", [P, T]), sb("nsc", [P, T]), sb("nbi", [P, T])
        lg, lm, lsum = sb("lg", [P, T, 3]), sb("lm", [P, T]), sb("lsum", [P, T])
        w = sb("w", [P, T, 3])
        den, den2, rdw = sb("den", [P, T]), sb("den2", [P, T]), sb("rdw", [P, T])

        block = ctx.enter_context(nc.Block())

        def loop(eng, body):
            with eng.Fori(0, NSEQ - 1) as i:
                for u in range(GPS):
                    body(i * GPS + u, u, i, False)
            for u in range(GPS):
                body((NSEQ - 1) * GPS + u, u, NSEQ - 1, u == GPS - 1)

        @block.sync
        def _(sp):
            def body(g, u, i, last):
                if u == 0 and not (isinstance(i, int) and i == NSEQ - 1):
                    for t in range(T):
                        wait(sp, f"h_in{t}", g + 1)
                    sp.dma_start(idx[:, :], x_idx[i + 1]).then_inc(idx_in, 16)
                for t in range(T):
                    wait(sp, "h_so", g, t)
                    wait(sp, "h_out", g, t)
                    sp.dma_start(h_mid[g, t], h[u][:, t, :]).then_inc(sem[f"h_stored{t}"], 16)
            loop(sp, body)
            for t in range(T):
                wait(sp, f"h_stored{t}", NSEQ * GPS - 1)

        @block.gpsimd
        def _(pool):
            def body(g, u, i, last):
                if not last:
                    if u == GPS - 1:
                        pool.wait_ge(idx_in, (i + 2) * 16)
                        waits_end(pool)
                    gather(pool, g + 1, (u + 1) % GPS)
                wait(pool, "a_lo", g)
                wait(pool, "small_ps", g)
                xf(g, 0)
                xf(g, 1)
                for t in range(T):
                    wait(pool, "n_var", g, t)
                    pool.tensor_tensor(nrs[:, t:t + 1], nv[:, t:t + 1], half[:, 0:1], ALU.pow).then_inc(sem["n_rstd"], 1)
                    if t == 0:
                        wait(pool, "rE_w", g)
                        wait(pool, "es_exp", g, 1)
                        wait(pool, "aT_ps", g - 1)
                        pool.tensor_tensor(
                            pr[:, :, 0:HS].rearrange("p t (h s) -> p t h s", h=H),
                            sx[:, :, 0:HS].rearrange("p t (h s) -> p t h s", h=H),
                            rs[:, :, 0:H].unsqueeze(3).to_broadcast([P, T, H, SE]), ALU.mult).then_inc(sem["probs"], 1)
                        for z in range(2):
                            pool.tensor_tensor(
                                pr[:, :, HS + z * SS:HS + (z + 1) * SS], sx[:, :, HS:WES],
                                rs[:, :, H:H + 1].to_broadcast([P, T, SS]), ALU.mult).then_inc(sem["probs"], 1)
                    if t == 1 and not last:
                        ln_scale(pool, g + 1)
                    if t == 2 and not last:
                        ln_rows(pool, g + 1, (u + 1) % GPS, (0, 1))
                if not last:
                    ln_rows(pool, g + 1, (u + 1) % GPS, (2, 3))
                for c in (2, 3):
                    wait(pool, "mix", g, c - 2)
                    xf(g, c)

            def xf(g, c):
                pool.tensor_tensor(xf_b[c % 2][:, :], xT_h[:, c, :].bitcast(F32), xT_l[:, c, :].bitcast(F32),
                                   ALU.add).then_inc(sem["xf"], 1)
            loop(pool, body)

        @block.scalar
        def _(act):
            def nT_hi(g, t):
                wait(act, "nT_ps", g, t)
                if t < 2:
                    wait(act, "num_ps", g, t + 2)
                else:
                    wait(act, "out_ps", g, t - 2)
                act.activation(nT_h[:, t % 2, :], ps(f"nT{t}")[:, :], ACT.Copy).then_inc(sem["nT_hi"], 1)

            def v_hi(g, t):
                wait(act, "v_ps", g, t)
                if t < 2:
                    wait(act, "out_ps", g - 1, t + 2)
                else:
                    wait(act, "num_ps", g, t - 2)
                act.activation(v_h[:, t % 2, :], ps(f"v{t}")[:, :], ACT.Copy).then_inc(sem["v_hi"], 1)

            def body(g, u, i, last):
                wait(act, "f_clip", g)
                act.activation(ef[M:P, :], ef[M:P, :], ACT.Exp, scale=-1.0).then_inc(sem["f_exp"], 1)
                wait(act, "u", g)
                act.activation(ef[M:P, :], ef[M:P, :], ACT.Ln).then_inc(sem["ln_u"], 1)
                wait(act, "l_clip", g, 1)
                act.activation(dec[:, :], dec[:, :], ACT.Exp, scale=sign[:, 0:1]).then_inc(sem["decay"], 1)
                wait(act, "qk_min", g)
                act.activation(qk[:, :], qk[:, :], ACT.Exp).then_inc(sem["qk_exp"], 1)
                wait(act, "fs_ps", g)
                wait(act, "small_ps", g - 1)
                act.activation(zc[:, :], ps("fs")[0:M, :], ACT.Copy).then_inc(sem["kS_sb"], 1)
                wait(act, "k_dec", g)
                wait(act, "a_ps", g - 1)
                act.activation(k_hl[0:M, :], kf[:, :], ACT.Copy).then_inc(sem["k_hi"], 1)
                act.activation(kh[:, :], kf[:, :], ACT.Copy).then_inc(sem["k_hi"], 1)
                wait(act, "e_ps", g)
                wait(act, "mix", g - 1, KB - 1)
                act.activation(am[:, :], ps("e")[:, :], ACT.Copy).then_inc(sem["e_sb"], 1)
                wait(act, "q_dup", g, 1)
                wait(act, "ret_ps", g - 1, KB - 1)
                act.activation(q2_h[:, :], q2[:, :], ACT.Copy).then_inc(sem["q_hi"], 1)
                wait(act, "c1_ps", g)
                act.activation(c1s[:, :], ps("c1")[:, :], ACT.Sigmoid, bias=c1b[:, 0:1]).then_inc(sem["c1_sig"], 1)
                v_hi(g, 0)
                wait(act, "es_sub", g, 0)
                act.activation(sx[:, :, HS:WES], sx[:, :, HS:WES], ACT.Exp).then_inc(sem["es_exp"], 1)
                v_hi(g, 1)
                wait(act, "kT_ps", g)
                wait(act, "state_ps", g - 1, T - 1)
                act.activation(flat(kT_hl[:, :, :]), ps("kT")[:, :], ACT.Copy).then_inc(sem["kT_sb"], 1)
                wait(act, "a_mask", g)
                wait(act, "out_ps", g - 1, T - 1)
                act.activation(a_h[:, :], am[:, :], ACT.Copy).then_inc(sem["a_hi"], 1)
                wait(act, "es_sub", g, 1)
                act.activation(sx[:, :, 0:HS], sx[:, :, 0:HS], ACT.Exp).then_inc(sem["es_exp"], 1)
                wait(act, "lg_sub", g)
                act.activation(flat(lg[:, :, :]), flat(lg[:, :, :]), ACT.Exp).then_inc(sem["w_exp"], 1)
                gate_sig(g, 0)
                for t in range(2):
                    s_hi(g, t)
                    v_hi(g, t + 2)
                    n_rows(g, t)
                s_hi(g, 2)
                nT_hi(g, 0)
                gate_sig(g, 1)
                n_rows(g, 2)
                wait(act, "sT_ps", g)
                act.activation(sT_h[:, :], ps("sT")[:, :], ACT.Copy).then_inc(sem["sT_hi"], 1)
                nT_hi(g, 1)
                wait(act, "aT_ps", g)
                act.activation(aT_h[:, :], ps("aT")[:, :], ACT.Copy).then_inc(sem["aT_hi"], 1)
                n_rows(g, 3)
                s_hi(g, 3)
                gate_sig(g, 2)
                mix_hi(g, 0)
                mix_hi(g, 1)
                gate_sig(g, 3)
                mix_hi(g, 2)
                mix_hi(g, 3)
                nT_hi(g, 2)
                nT_hi(g, 3)
                if not last:
                    xT_hi(act, g + 1)

            def s_hi(g, t):
                wait(act, "state_ps", g, t)
                act.activation(s_h[:, :], state[:, :], ACT.Copy).then_inc(sem["s_hi"], 1)

            def n_rows(g, t):
                wait(act, "n_bias", g, t)
                if t >= 2:
                    wait(act, "nT_ps", g, t - 2)
                else:
                    wait(act, "nT_ps", g - 1, t + 2)
                act.activation(n[:, t % 2, :], ps(f"num{t}")[:, :], ACT.Identity, bias=nbi[:, t:t + 1],
                               scale=nsc[:, t:t + 1]).then_inc(sem["n_rows"], 1)

            def gate_sig(g, c):
                wait(act, "gate_ps", g, c)
                if c >= 2:
                    wait(act, "mix_mul", g, c - 2)
                act.activation(gate_b[c % 2][:, :], ps(f"gate{c}")[:, :], ACT.Sigmoid,
                               bias=sgb[:, c:c + 1]).then_inc(sem["gate"], 1)

            def mix_hi(g, c):
                wait(act, "mix", g, c)
                if c == 0:
                    wait(act, "so_ps", g - 1, T - 1)
                act.activation(mixT_h[:, c, :], mix_b[c % 2][:, :], ACT.Copy).then_inc(sem["mix_hi"], 1)
            loop(act, body)

        @block.tensor
        def _(pe):
            def by_feature(g, use, signal, wh, wl):
                bank_free(pe, use, g)
                for k in range(KB):
                    last = split3(pe, ps(use)[:, :], wh(k), wl(k), xT_h[:, k, :], xT_l[:, k, :], k == 0, k == KB - 1)
                last.then_inc(sem[signal], 1)

            def v_rows(g, t):
                bank_free(pe, f"v{t}", g)
                for k in range(KB):
                    last = split3(pe, ps(f"v{t}")[:, :], xT_h[:, k, t * P:(t + 1) * P], xT_l[:, k, t * P:(t + 1) * P],
                                  w_hi["v"][:, k, :], w_lo["v"][:, k, :], k == 0, k == KB - 1)
                last.then_inc(sem["v_ps"], 1)

            def nT(g, t):
                wait(pe, "n_rows", g, t)
                bank_free(pe, f"nT{t}", g)
                for k in range(KB):
                    last = pe.transpose(ps(f"nT{t}")[:, k * P:(k + 1) * P], n[:, t % 2, k * P:(k + 1) * P], ident[:, :])
                last.then_inc(sem["nT_ps"], 1)

            def out_rows(g, t):
                wait(pe, "nT_lo", g, t)
                bank_free(pe, f"out{t}", g)
                o = ps(f"out{t}")[:, :]
                cols = slice(t * P, (t + 1) * P)
                split3(pe, o, aT_h[:, cols], aT_l[:, cols], w_hi["ve"][:, :], w_lo["ve"][:, :], True, False)
                for k in range(KB):
                    blk = slice(k * P, (k + 1) * P)
                    last = split3(pe, o, nT_h[:, t % 2, blk], nT_l[:, t % 2, blk], w_hi["wo"][:, k, :], w_lo["wo"][:, k, :],
                                  False, k == KB - 1)
                last.then_inc(sem["out_ps"], 1)

            def body(g, u, i, last_group):
                wait(pe, "xT_lo", g, T - 1)
                by_feature(g, "fs", "fs_ps", lambda k: w_hi["qkf"][:, k, 2 * M:], lambda k: w_lo["qkf"][:, k, 2 * M:])
                by_feature(g, "c1", "c1_ps", lambda k: w_hi["c1"][:, k, :], lambda k: w_lo["c1"][:, k, :])
                by_feature(g, "qk", "qk_ps", lambda k: w_hi["qkf"][:, k, 0:2 * M], lambda k: w_lo["qkf"][:, k, 0:2 * M])
                by_feature(g, "e", "e_ps", lambda k: w_hi["se"][:, k, :], lambda k: w_lo["se"][:, k, :])
                v_rows(g, 0)
                wait(pe, "e_sb", g)
                bank_free(pe, "eT", g)
                for t in range(T):
                    last = pe.transpose(ps("eT")[:, t * P:(t + 1) * P], am[:, t * P:(t + 1) * P], ident[:, :])
                last.then_inc(sem["eT_ps"], 1)
                wait(pe, "kS_sb", g)
                bank_free(pe, "kS", g)
                waits_end(pe)
                for t in range(T):
                    last = pe.transpose(ps("kS")[:, t * SS:(t + 1) * SS], zc[:, t * P:(t + 1) * P], ident[0:SS, 0:SS])
                last.then_inc(sem["kS_ps"], 1)
                v_rows(g, 1)
                wait(pe, "k_lo", g)
                bank_free(pe, "kT", g)
                for t in range(T):
                    last = pe.transpose(ps("kT")[:, t * P:(t + 1) * P], k_hl[:, t * P:(t + 1) * P].bitcast(F32), ident[:, :])
                last.then_inc(sem["kT_ps"], 1)
                wait(pe, "q_lo", g)
                bank_free(pe, "a", g)
                for t in range(T):
                    cols = slice(t * P, (t + 1) * P)
                    pe.matmul(ps("a")[:, cols], k_hl[:, cols], q2_h[:, cols], start=True, stop=False)
                    last = pe.matmul(ps("a")[:, cols], k_hl[:, cols], q2_l[:, cols], start=False, stop=True)
                last.then_inc(sem["a_ps"], 1)
                wait(pe, "silu", g)
                wait(pe, "qz", g)
                wait(pe, "es_sub", g, 0)
                for t in range(T):
                    pe.matmul(ps("small")[:, 4 * t:4 * t + 3], c1s[:, t * P:(t + 1) * P], c2w[:, :], start=True, stop=True)
                    last = pe.matmul(ps("small")[:, 4 * t + 3:4 * t + 4], zc[:, t * P:(t + 1) * P], ones[0:M, :],
                                     start=True, stop=True)
                last.then_inc(sem["small_ps"], 1)

                def gate(c):
                    blk = slice(c * P, (c + 1) * P)
                    by_feature(g, f"gate{c}", "gate_ps", lambda k: w_hi["sg"][:, k, blk], lambda k: w_lo["sg"][:, k, blk])

                def retrieved(c):
                    blk = slice(c * P, (c + 1) * P)
                    bank_free(pe, f"ret{c}", g)
                    pe.matmul(ps(f"ret{c}")[:, :], know_hl[:, blk], sT_h[:, :], start=True, stop=False)
                    pe.matmul(ps(f"ret{c}")[:, :], know_hl[:, blk], sT_l[:, :], start=False, stop=True)\
                        .then_inc(sem["ret_ps"], 1)

                gate(0)
                for t in range(T):
                    cols = slice(t * P, (t + 1) * P)
                    o = ps(f"num{t}")[:, :]
                    bank_free(pe, f"num{t}", g)
                    first = u == 0 and t == 0
                    if not first:
                        wait(pe, "s_lo", g if t else g - 1, t - 1 if t else T - 1)
                        split3(pe, o, q2_h[:, cols], q2_l[:, cols], s_h[:, :], s_l[:, :], True, False)
                    wait(pe, "kT_sb", g)
                    wait(pe, "v_lo", g, t)
                    if first:
                        wait(pe, "s_lo", g - 1, T - 1)
                    pe.matmul(state[:, :], kT_hl[:, t, :], v_h[:, t % 2, :], start=first, stop=False, skip_group_check=True)
                    pe.matmul(state[:, :], kT_hl[:, t, :], v_l[:, t % 2, :], start=False, stop=True,
                              skip_group_check=True).then_inc(sem["state_ps"], 1)
                    if t == 0:
                        wait(pe, "a_lo", g)
                    split3(pe, o, a_h[:, cols], a_l[:, cols], v_h[:, t % 2, :], v_l[:, t % 2, :], first, True)\
                        .then_inc(sem["num_ps"], 1)
                    if t < 2:
                        v_rows(g, t + 2)
                    elif t == 2:
                        nT(g, 0)
                        gate(1)
                        nT(g, 1)
                wait(pe, "probs", g, 2)
                bank_free(pe, "sT", g)
                for t in range(T):
                    last = pe.transpose(ps("sT")[:, t * P:(t + 1) * P], pr[:, t, P:2 * P], ident[:, :])
                last.then_inc(sem["sT_ps"], 1)
                bank_free(pe, "aT", g)
                for t in range(T):
                    last = pe.transpose(ps("aT")[:, t * P:(t + 1) * P], pr[:, t, 0:P], ident[:, :])
                last.then_inc(sem["aT_ps"], 1)
                gate(2)
                wait(pe, "sT_lo", g)
                retrieved(0)
                retrieved(1)
                gate(3)
                retrieved(2)
                retrieved(3)
                wait(pe, "aT_lo", g)
                out_rows(g, 0)
                nT(g, 2)
                out_rows(g, 1)
                nT(g, 3)
                wait(pe, "mix_lo", g, KB - 1)
                for t in range(T):
                    cols = slice(t * P, (t + 1) * P)
                    bank_free(pe, f"so{t}", g)
                    for k in range(KB):
                        last = split3(pe, ps(f"so{t}")[:, :], mixT_h[:, k, cols], mixT_l[:, k, cols], w_hi["so"][:, k, :],
                                      w_lo["so"][:, k, :], k == 0, k == KB - 1)
                    last.then_inc(sem["so_ps"], 1)
                if not last_group:
                    xT(pe, g + 1, g)
                out_rows(g, 2)
                out_rows(g, 3)
            loop(pe, body)

        @block.vector
        def _(dve):
            def v_lo(g, t):
                wait(dve, "v_hi", g, t)
                done(dve.tensor_tensor(v_l[:, t % 2, :], ps(f"v{t}")[:, :], v_h[:, t % 2, :].bitcast(F32),
                                       ALU.subtract), "v_lo")

            def nT_lo(g, t):
                wait(dve, "nT_hi", g, t)
                done(dve.tensor_tensor(nT_l[:, t % 2, :], ps(f"nT{t}")[:, :], nT_h[:, t % 2, :].bitcast(F32),
                                       ALU.subtract), "nT_lo")

            def slot_scores(g):
                eE = ps("eT")[:, :].rearrange("p (t h s) -> p t h s", t=T, h=H)
                wait(dve, "eT_ps", g)
                done(dve.tensor_reduce(mE[:, :, :], eE, AX.X, ALU.max), "es_max")
                wait(dve, "es_max", g, 1)
                done(dve.tensor_tensor(sx[:, :, 0:HS].rearrange("p t (h s) -> p t h s", h=H), eE,
                                       mE[:, :, :].unsqueeze(3).to_broadcast([P, T, H, SE]), ALU.subtract), "es_sub")

            def know_scores(g):
                e2 = ps("kS")[:, 0:T * SS].rearrange("p (t n) -> p t n", t=T)
                wait(dve, "kS_ps", g)
                wait(dve, "probs", g - 1, 2)
                done(dve.tensor_reduce(mS[:, :], e2, AX.X, ALU.max), "es_max")
                wait(dve, "es_max", g, 0)
                done(dve.tensor_tensor(sx[:, :, HS:WES], e2, mS[:, :].unsqueeze(2).to_broadcast([P, T, SS]),
                                       ALU.subtract), "es_sub")

            def body(g, u, i, last):
                wait(dve, "fs_ps", g)
                wait(dve, "mix", g - 1, KB - 1)
                done(dve.tensor_scalar(ef[M:P, :], ps("fs")[M:P, :], bff[M:P, 0:1], F_CLIP, ALU.add, ALU.max), "f_clip")
                wait(dve, "f_exp", g)
                done(dve.tensor_scalar(ef[M:P, :], ef[M:P, :], 1.0, 1.0 / FORGET_MIN, ALU.add, ALU.min), "u")
                wait(dve, "ln_u", g)
                wait(dve, "l_carry", g - 1)
                done(dve.tensor_tensor_scan(lraw[M:P, :], ones[M:P, :].to_broadcast([M, GT]), ef[M:P, :],
                                            carry[M:P, 0:1] if u else 0.0, ALU.mult, ALU.subtract), "lsum_raw")
                wait(dve, "lsum_raw", g)
                for z in range(2):
                    done(dve.tensor_scalar(dec[z * M:(z + 1) * M, :], lraw[M:P, :], -LOG_CLIP, LOG_CLIP, ALU.max, ALU.min),
                         "l_clip")
                done(dve.tensor_copy(carry[M:P, 0:1], lraw[M:P, GT - 1:GT]), "l_carry")
                wait(dve, "qk_ps", g)
                wait(dve, "mix_lo", g - 1, KB - 1)
                done(dve.tensor_scalar(qk[:, :], ps("qk")[:, :], 0.0, None, ALU.min), "qk_min")
                wait(dve, "qk_exp", g)
                done(dve.scalar_tensor_tensor(qk[:, :], ps("qk")[:, :], 0.0, qk[:, :], ALU.max, ALU.add), "qk_elu")
                wait(dve, "decay", g)
                wait(dve, "qk_elu", g)
                wait(dve, "k_lo", g - 1)
                done(dve.tensor_tensor(kf[:, :], qk[M:2 * M, :], dec[M:2 * M, :], ALU.mult), "k_dec")
                wait(dve, "q_lo", g - 1)
                for z in range(2):
                    done(dve.scalar_tensor_tensor(q2[z * M:(z + 1) * M, :], qk[0:M, :], Q_SCALE, dec[0:M, :], ALU.mult,
                                                  ALU.mult), "q_dup")
                wait(dve, "k_hi", g, 1)
                done(dve.tensor_tensor(k_hl[M:2 * M, :], kf[:, :], kh[:, :].bitcast(F32), ALU.subtract), "k_lo")
                wait(dve, "q_hi", g)
                done(dve.tensor_tensor(q2_l[:, :], q2[:, :], q2_h[:, :].bitcast(F32), ALU.subtract), "q_lo")
                know_scores(g)
                wait(dve, "c1_sig", g)
                done(dve.scalar_tensor_tensor(c1s[:, :], ps("c1")[:, :], c1b[:, 0:1], c1s[:, :], ALU.add, ALU.mult), "silu")
                wait(dve, "kS_ps", g)
                wait(dve, "z_carry", g - 1)
                done(dve.tensor_tensor_scan(zc[:, :], ones[0:M, :].to_broadcast([M, GT]), kf[:, :],
                                            carry[0:M, 1:2] if u else 0.0, ALU.mult, ALU.add), "z_sum")
                wait(dve, "z_sum", g)
                done(dve.tensor_copy(carry[0:M, 1:2], zc[:, GT - 1:GT]), "z_carry")
                wait(dve, "z_carry", g)
                wait(dve, "q_dup", g, 0)
                done(dve.tensor_tensor(zc[:, :], zc[:, :], q2[0:M, :], ALU.mult), "qz")
                v_lo(g, 0)
                slot_scores(g)
                wait(dve, "a_ps", g)
                done(dve.tensor_tensor(am[:, :].rearrange("p (t n) -> p t n", t=T),
                                       ps("a")[:, :].rearrange("p (t n) -> p t n", t=T),
                                       causal[:, :].unsqueeze(1).to_broadcast([P, T, P]), ALU.mult), "a_mask")
                v_lo(g, 1)
                wait(dve, "a_hi", g)
                done(dve.tensor_tensor(a_l[:, :], am[:, :], a_h[:, :].bitcast(F32), ALU.subtract), "a_lo")
                wait(dve, "es_exp", g, 1)
                done(dve.tensor_reduce(rs[:, :, 0:H], sx[:, :, 0:HS].rearrange("p t (h s) -> p t h s", h=H), AX.X,
                                       ALU.add), "es_sum")
                done(dve.tensor_reduce(rs[:, :, H], sx[:, :, HS:WES], AX.X, ALU.add), "es_sum")
                wait(dve, "es_sum", g, 1)
                done(dve.reciprocal(flat(rs[:, :, :]), flat(rs[:, :, :])), "es_rec")
                wait(dve, "small_ps", g)
                small = ps("small")[:, 0:4 * T].rearrange("p (t n) -> p t n", t=T)
                done(dve.tensor_tensor(lg[:, :, :], small[:, :, 0:3], c2b[:, :].unsqueeze(1).to_broadcast([P, T, 3]),
                                       ALU.add), "lg_add")
                done(dve.tensor_scalar(den[:, :], small[:, :, 3], DEN_EPS, None, ALU.add), "den_add")
                wait(dve, "lg_add", g)
                done(dve.tensor_reduce(lm[:, :], lg[:, :, :], AX.X, ALU.max), "lg_max")
                wait(dve, "den_add", g)
                done(dve.reciprocal(den[:, :], den[:, :]), "den_rec")
                wait(dve, "lg_max", g)
                done(dve.tensor_tensor(lg[:, :, :], lg[:, :, :], lm[:, :].unsqueeze(2).to_broadcast([P, T, 3]),
                                       ALU.subtract), "lg_sub")
                wait(dve, "den_rec", g)
                done(dve.tensor_tensor(den2[:, :], den[:, :], den[:, :], ALU.mult), "den_sq")
                wait(dve, "w_exp", g)
                done(dve.tensor_reduce(lsum[:, :], lg[:, :, :], AX.X, ALU.add), "w_sum")
                wait(dve, "w_sum", g)
                done(dve.reciprocal(lsum[:, :], lsum[:, :]), "w_rec")
                wait(dve, "w_rec", g)
                done(dve.tensor_tensor(w[:, :, :], lg[:, :, :], lsum[:, :].unsqueeze(2).to_broadcast([P, T, 3]),
                                       ALU.mult), "w_done")
                wait(dve, "w_done", g)
                wait(dve, "es_rec", g)
                done(dve.tensor_tensor(rs[:, :, 0:H], rs[:, :, 0:H], w[:, :, 1:2].to_broadcast([P, T, H]), ALU.mult), "rE_w")
                done(dve.tensor_tensor(rdw[:, :], den[:, :], w[:, :, 0], ALU.mult), "rd_w")
                for t in range(T):
                    if t < 3:
                        s_lo(g, t)
                    wait(dve, "num_ps", g, t)
                    done(dve.bn_stats(nb6[:, t, :], ps(f"num{t}")[:, :]), "n_bn")
                    wait(dve, "n_bn", g, t)
                    waits_end(dve)
                    done(dve.bn_aggr(nmv[:, t, :], nb6[:, t, :]), "n_stats")
                    wait(dve, "n_stats", g, t)
                    wait(dve, "den_sq", g)
                    done(dve.tensor_scalar(nv[:, t:t + 1], nmv[:, t, 1:2], den2[:, t:t + 1], LN_EPS, ALU.mult, ALU.add),
                         "n_var")
                    if t < 2:
                        v_lo(g, t + 2)
                    elif t == 2:
                        nT_lo(g, 0)
                    else:
                        wait(dve, "sT_hi", g)
                        done(dve.tensor_tensor(sT_l[:, :], ps("sT")[:, :], sT_h[:, :].bitcast(F32), ALU.subtract), "sT_lo")
                    wait(dve, "n_rstd", g, t)
                    wait(dve, "rd_w", g)
                    done(dve.tensor_tensor(nsc[:, t:t + 1], nrs[:, t:t + 1], rdw[:, t:t + 1], ALU.mult), "n_scale")
                    wait(dve, "n_scale", g, t)
                    done(dve.scalar_tensor_tensor(nbi[:, t:t + 1], nmv[:, t, 0:1], -1.0, nsc[:, t:t + 1], ALU.mult,
                                                  ALU.mult), "n_bias")
                    if t < 2 and not last:
                        ln_stats(dve, g + 1, (u + 1) % GPS, (2 * t, 2 * t + 1))
                    if t == 2:
                        if not last:
                            ln_bias(dve, g + 1)
                        xg(g, 0)
                nT_lo(g, 1)
                wait(dve, "aT_hi", g)
                done(dve.tensor_tensor(aT_l[:, :], ps("aT")[:, :], aT_h[:, :].bitcast(F32), ALU.subtract), "aT_lo")
                xg(g, 1)
                s_lo(g, 3)
                mix_mul(g, 0)
                mix(g, 0)
                mix_mul(g, 1)
                mix(g, 1)
                mix_lo(g, 0)
                xg(g, 2)
                mix_mul(g, 2)
                mix_lo(g, 1)
                mix(g, 2)
                xg(g, 3)
                mix_mul(g, 3)
                mix_lo(g, 2)
                mix(g, 3)
                mix_lo(g, 3)
                h_bias(g, u, 0)
                h_bias(g, u, 1)
                h_out(g, u, 0)
                nT_lo(g, 2)
                h_out(g, u, 1)
                nT_lo(g, 3)
                h_bias(g, u, 2)
                h_so(g, u, 0)
                h_bias(g, u, 3)
                for t in range(1, T):
                    h_so(g, u, t)
                if not last:
                    xT_lo(dve, g + 1)
                h_out(g, u, 2)
                h_out(g, u, 3)

            def s_lo(g, t):
                wait(dve, "s_hi", g, t)
                done(dve.tensor_tensor(s_l[:, :], state[:, :], s_h[:, :].bitcast(F32), ALU.subtract), "s_lo")

            def xg(g, c):
                wait(dve, "xf", g, c)
                wait(dve, "gate", g, c)
                done(dve.scalar_tensor_tensor(xf_b[c % 2][:, :], gate_b[c % 2][:, :], 1.0, xf_b[c % 2][:, :],
                                              ALU.subtract, ALU.mult), "xg")

            def mix_mul(g, c):
                wait(dve, "ret_ps", g, c)
                wait(dve, "gate", g, c)
                if c >= 2:
                    wait(dve, "mix_lo", g, c - 2)
                done(dve.tensor_tensor(mix_b[c % 2][:, :], ps(f"ret{c}")[:, :], gate_b[c % 2][:, :], ALU.mult), "mix_mul")

            def mix(g, c):
                wait(dve, "mix_mul", g, c)
                wait(dve, "xg", g, c)
                done(dve.tensor_tensor(mix_b[c % 2][:, :], mix_b[c % 2][:, :], xf_b[c % 2][:, :], ALU.subtract), "mix")

            def mix_lo(g, c):
                wait(dve, "mix_hi", g, c)
                done(dve.tensor_tensor(mixT_l[:, c, :], mix_b[c % 2][:, :], mixT_h[:, c, :].bitcast(F32), ALU.subtract),
                     "mix_lo")

            def h_bias(g, u, t):
                done(dve.scalar_tensor_tensor(h[u][:, t, :], bias_wo[:, :], w[:, t, 0:1], h[u][:, t, :],
                                              ALU.mult, ALU.add), "h_bias")

            def h_so(g, u, t):
                wait(dve, "so_ps", g, t)
                if t < 2:
                    wait(dve, "h_out", g, t)
                else:
                    wait(dve, "h_bias", g, t)
                done(dve.scalar_tensor_tensor(h[u][:, t, :], ps(f"so{t}")[:, :], w[:, t, 2:3], h[u][:, t, :],
                                              ALU.mult, ALU.add), "h_so")

            def h_out(g, u, t):
                wait(dve, "out_ps", g, t)
                if t < 2:
                    wait(dve, "h_bias", g, t)
                else:
                    wait(dve, "h_so", g, t)
                done(dve.tensor_tensor(h[u][:, t, :], ps(f"out{t}")[:, :], h[u][:, t, :], ALU.add), "h_out")

            loop(dve, body)


def prep_a(nc, e, r):
    bank, ident, half, blocks = e["bank"], e["ident"], e["half"], e["blocks"]
    (D, KB, M, SE, SS, H, HD, HS) = (r.get(n, e.get(n)) for n in ("D", "KB", "M", "SE", "SS", "H", "HD", "HS"))
    know_hl, ones, full, w_hi, w_lo, credit = (r[n] for n in ("know_hl", "ones", "full", "w_hi", "w_lo", "credit"))
    with nc.cleanup_on_exit(), ExitStack() as ctx:
        def sb(name, shape, dt=F32):
            return ctx.enter_context(nc.sbuf_tensor(name, shape, dt))

        def new(name):
            return nc.alloc_semaphore("PA_" + name)

        raw = {n: sb("raw_" + n, [P, KB, D]) for n in ("Eq", "Sin", "Ek", "Ev", "Eo")}
        raw_es, raw_kn = sb("raw_es", [SE, D]), sb("raw_kn", [P, D])
        EqT, SinT = sb("EqT", [P, H, D]), sb("SinT", [P, KB, D])
        esT, knT = sb("esT", [P, KB, SE]), sb("knT", [P, KB, SS])
        khT = sb("khT", [P, H, SE])
        vhT = sb("vhT", [P, H, HS])
        kn_hi = sb("kn_hi", [P, D], F32R)
        lng, lnb, lnb_w = sb("lng", [P, KB]), sb("lnb", [P, KB]), sb("lnb_w", [P, KB, P])
        one_mat = sb("one_mat", [P, P])

        LOADS = ("Eq", "Sin", "Ek", "Ev", "Eo", "Wo", "Wv", "Sg_w", "So", "qkf", "c1", "es", "kn", "ln", "small")
        loads = {n: new("in_" + n) for n in LOADS}
        zeroed, ident_ok, causal_ok = new("zeroed"), new("ident_ok"), new("causal_ok")
        small_T, small_sb = new("small_T"), new("small_sb")
        big_T, big_sb = new("big_T"), new("big_sb")
        heads, heads_sb = new("heads"), new("heads_sb")
        folded, folded_sb = new("folded"), new("folded_sb")
        lnb_sb, wo_row, wo_row_sb, wo_g = new("lnb_sb"), new("wo_row"), new("wo_row_sb"), new("wo_g")
        hi, lo = new("hi"), new("lo")
        kn_split, signed = new("kn_split"), new("signed")

        SPLITS = [("c1", [(loads["c1"], 16)]), ("v", [(loads["Wv"], 16)]), ("sg", [(loads["Sg_w"], 16)]),
                  ("so", [(loads["So"], 16)]), ("wo", [(wo_g, KB)]), ("se", [(folded_sb, 1)]),
                  ("qkf", [(loads["qkf"], 48), (folded_sb, 2)]), ("ve", [(folded_sb, 3)])]

        block = ctx.enter_context(nc.Block())

        @block.sync
        def _(sp):
            credit(sp, [f"h_stored{t}" for t in range(T)], 16)
            sp.dma_start(r["idx"][:, :], r["x_idx"][0]).then_inc(r["idx_in"], 16)
            sp.dma_start(raw_es[:, :], e["eslots"][0]).then_inc(loads["es"], 16)
            sp.dma_start(raw_kn[0:SS, :], e["know"][0]).then_inc(loads["kn"], 16)
            sp.dma_start(raw_kn[SS:2 * SS, :], e["know"][0]).then_inc(loads["kn"], 16)
            for n, o in (("Ek", raw["Ek"]), ("Ev", raw["Ev"]), ("Wv", full["v"]), ("Eo", raw["Eo"])):
                sp.dma_start(o[:, :, :], blocks(e[n])).then_inc(loads[n], 16)
            for j, n in ((0, "Wq"), (1, "Wk"), (3, "Wf")):
                sp.dma_start(full["qkf"][:, :, j * M:(j + 1) * M], blocks(e[n])).then_inc(loads["qkf"], 16)
            sp.dma_start(full["so"][:, :, :], blocks(e["So"])).then_inc(loads["So"], 16)

        @block.scalar
        def _(act):
            credit(act, r["BY_ACT"])
            act.dma_start(raw["Eq"][:, :, :], blocks(e["Eq"])).then_inc(loads["Eq"], 16)
            act.dma_start(full["c1"][:, :, :], blocks(e["C1w"])).then_inc(loads["c1"], 16)
            for n, o in (("Sin", raw["Sin"]), ("Wo", full["wo"]), ("Sg_w", full["sg"])):
                act.dma_start(o[:, :, :], blocks(e[n])).then_inc(loads[n], 16)
            for j in range(2 * KB):
                act.wait_ge(big_T, j + 1)
                dst = (EqT if j < KB else SinT)[:, j % KB, :]
                act.activation(dst, bank[j % 4][:, :], ACT.Copy).then_inc(big_sb, 1)
            act.wait_ge(heads, 1)
            act.activation(khT[:, :, :].rearrange("p h s -> p (h s)"), bank[4][:, 0:HS], ACT.Copy).then_inc(heads_sb, 1)

            def folded_out(k, out, o, n, scale):
                act.wait_ge(folded, k + 1)
                act.activation(out, o.rearrange("p (k n) -> p k n", n=n), ACT.Copy, scale=scale).then_inc(folded_sb, 1)

            for n, ready in SPLITS:
                if n == "se":
                    folded_out(0, full["se"][:, :, :], bank[5][:, 0:KB * HS], HS, float(HD) ** -0.5)
                elif n == "qkf":
                    folded_out(1, full["qkf"][:, :, 2 * M:3 * M], bank[6][:, 0:KB * SS], SS, float(D) ** -0.5)
                elif n == "ve":
                    act.wait_ge(folded, 3)
                    act.activation(full["ve"][:, :], bank[7][:, :], ACT.Copy).then_inc(folded_sb, 1)
                for signal, value in ready:
                    act.wait_ge(signal, value)
                act.activation(w_hi[n][:], full[n][:], ACT.Copy).then_inc(hi, 1)
            r["xT_hi"](act, 0)

        @block.gpsimd
        def _(pool):
            credit(pool, r["BY_POOL"])
            for a, v in ((ident, 0.0), (one_mat, 1.0), (half, -0.5), (ones, 1.0), (vhT, 0.0)):
                pool.memset(a[:], v).then_inc(zeroed, 1)
            pool.wait_ge(zeroed, 5)
            pool.affine_select(out=ident[:, :], in_=ident[:, :], compare_op=ALU.not_equal, fill=1.0, base=0,
                               pattern=[[-1, P]], channel_multiplier=1).then_inc(ident_ok, 1)
            pool.dma_start(lng[:, :], e["ln_g"].rearrange("(k p) -> p k", p=P), allow_slow_non_contiguous=True).then_inc(loads["ln"], 16)
            pool.dma_start(lnb[:, :], e["ln_b"].rearrange("(k p) -> p k", p=P), allow_slow_non_contiguous=True).then_inc(loads["ln"], 16)
            pool.wait_ge(r["idx_in"], 16)
            r["gather"](pool, 0, 0)
            pool.affine_select(out=r["causal"][:, :], in_=one_mat[:, :], compare_op=ALU.is_ge, fill=0.0, base=0,
                               pattern=[[1, P]], channel_multiplier=-1).then_inc(causal_ok, 1)
            pool.dma_start(r["c1b"][:, :], e["C1b"].rearrange("(p a) -> p a", a=1), allow_slow_non_contiguous=True).then_inc(loads["small"], 16)
            pool.dma_start(r["sgb"][:, :], e["Sg_b"].rearrange("(k p) -> p k", p=P), allow_slow_non_contiguous=True).then_inc(loads["small"], 16)
            pool.dma_start(r["c2w"][:, :], e["C2w"]).then_inc(loads["small"], 16)
            pool.dma_start(r["c2b"][:, :], e["C2b"].rearrange("(a n) -> a n", a=1).to_broadcast([P, 3])).then_inc(loads["small"], 16)
            pool.dma_start(r["bff"][M:P, :], e["bf"].rearrange("(p a) -> p a", a=1), allow_slow_non_contiguous=True).then_inc(loads["small"], 16)
            r["ln_scale"](pool, 0)
            r["ln_rows"](pool, 0, 0, range(T))
            pool.wait_ge(loads["small"], 80)

        @block.tensor
        def _(pe):
            credit(pe, r["BY_PE"])
            pe.wait_ge(ident_ok, 1)
            pe.wait_ge(loads["es"], 16)
            for k in range(KB):
                last = pe.transpose(bank[4][:, k * SE:(k + 1) * SE], raw_es[:, k * P:(k + 1) * P], ident[0:SE, 0:SE])
            last.then_inc(small_T, 1)
            pe.wait_ge(loads["kn"], 32)
            for k in range(KB):
                last = pe.transpose(bank[5][:, k * SS:(k + 1) * SS], raw_kn[0:SS, k * P:(k + 1) * P], ident[0:SS, 0:SS])
            last.then_inc(small_T, 1)
            for j in range(2 * KB):
                n, blk = ("Eq", j) if j < KB else ("Sin", j - KB)
                pe.wait_ge(loads[n], 16)
                if j >= 4:
                    pe.wait_ge(big_sb, j - 3)
                for k in range(KB):
                    last = pe.transpose(bank[j % 4][:, k * P:(k + 1) * P], raw[n][:, k, blk * P:(blk + 1) * P], ident[:, :])
                last.then_inc(big_T, 1)
            pe.wait_ge(small_sb, 2)
            for n, o in (("Ek", bank[4]), ("Ev", bank[5])):
                pe.wait_ge(loads[n], 16)
                for hd in range(H):
                    for k in range(KB):
                        last = pe.matmul(o[:, hd * SE:(hd + 1) * SE], raw[n][:, k, hd * HD:(hd + 1) * HD], esT[:, k, :],
                                         start=k == 0, stop=k == KB - 1)
                last.then_inc(heads, 1)
            pe.wait_ge(lnb_sb, 1)
            pe.wait_ge(big_sb, 2 * KB)
            pe.wait_ge(loads["Wo"], 16)
            for k in range(KB):
                last = pe.matmul(bank[0][:, :], lnb_w[:, k, :], full["wo"][:, k, :], start=k == 0, stop=k == KB - 1)
            last.then_inc(wo_row, 1)
            pe.wait_ge(heads_sb, 2)
            for k in range(KB):
                for hd in range(H):
                    last = pe.matmul(bank[5][:, k * HS + hd * SE:k * HS + (hd + 1) * SE], EqT[:, hd, k * P:(k + 1) * P],
                                     khT[:, hd, :], start=True, stop=True)
            last.then_inc(folded, 1)
            for k in range(KB):
                for b in range(KB):
                    last = pe.matmul(bank[6][:, k * SS:(k + 1) * SS], SinT[:, b, k * P:(k + 1) * P], knT[:, b, :],
                                     start=b == 0, stop=b == KB - 1)
            last.then_inc(folded, 1)
            pe.wait_ge(loads["Eo"], 16)
            for hd in range(H):
                last = pe.matmul(bank[7][:, :], vhT[:, hd, :], raw["Eo"][:, hd, :], start=hd == 0, stop=hd == H - 1)
            last.then_inc(folded, 1)
            r["xT"](pe, 0, -1)

        @block.vector
        def _(dve):
            credit(dve, r["BY_DVE"])
            dve.memset(r["sign"][0:M, :], 1.0).then_inc(signed, 1)
            dve.memset(r["sign"][M:P, :], -1.0).then_inc(signed, 1)
            dve.wait_ge(small_T, 1)
            dve.tensor_copy(esT[:, :, :].rearrange("p k n -> p (k n)"), bank[4][:, 0:KB * SE]).then_inc(small_sb, 1)
            dve.wait_ge(small_T, 2)
            dve.tensor_copy(knT[:, :, :].rearrange("p k n -> p (k n)"), bank[5][:, 0:KB * SS]).then_inc(small_sb, 1)
            dve.wait_ge(loads["kn"], 32)
            dve.tensor_copy(know_hl[0:SS, :], raw_kn[0:SS, :]).then_inc(kn_split, 1)
            dve.tensor_copy(kn_hi[SS:P, :], raw_kn[SS:P, :]).then_inc(kn_split, 1)
            dve.wait_ge(kn_split, 2)
            dve.tensor_tensor(know_hl[SS:P, :], raw_kn[SS:P, :], kn_hi[SS:P, :].bitcast(F32), ALU.subtract).then_inc(kn_split, 1)
            dve.wait_ge(loads["ln"], 32)
            dve.tensor_copy(lnb_w[:, :, :], lnb[:, :].unsqueeze(2).to_broadcast([P, KB, P])).then_inc(lnb_sb, 1)
            dve.wait_ge(zeroed, 5)
            dve.wait_ge(heads, 2)
            dve.wait_ge(heads_sb, 1)
            for hd in range(H):
                last = dve.tensor_copy(vhT[:, hd, hd * SE:(hd + 1) * SE], bank[5][:, hd * SE:(hd + 1) * SE])
            last.then_inc(heads_sb, 1)
            def split_lo(k):
                n, _ = SPLITS[k]
                dve.wait_ge(hi, k + 1)
                dve.tensor_tensor(w_lo[n][:], full[n][:], w_hi[n][:].bitcast(F32), ALU.subtract).then_inc(lo, 1)
            for k in range(len(SPLITS)):
                if SPLITS[k][0] == "so":
                    dve.wait_ge(wo_row, 1)
                    dve.tensor_copy(r["bias_wo"][:, :], bank[0][:, :]).then_inc(wo_row_sb, 1)
                    for b in range(KB):
                        dve.tensor_scalar(full["wo"][:, b, :], full["wo"][:, b, :], lng[:, b:b + 1], None,
                                          ALU.mult).then_inc(wo_g, 1)
                split_lo(k)
                if SPLITS[k][0] == "sg":
                    r["ln_stats"](dve, 0, 0, range(T))
                    r["ln_bias"](dve, 0)
            r["xT_lo"](dve, 0)
            dve.wait_ge(lo, len(SPLITS))
            dve.wait_ge(signed, 2)




def pass_b(nc, e):
    (bank, ident, half, blocks, split3) = (e[n] for n in ("bank", "ident", "half", "blocks", "split3"))
    NSEQ, D, KB, NE, GPS = (e[n] for n in ("NSEQ", "D", "KB", "NE", "GPS"))
    h_mid, out_g = e["h_mid"], e["out_g"]
    NS = e["sw1"].shape[1] // P
    NC = NS + NE
    KC = 32
    R1 = 3 * NE
    NBUF = 4

    c_rows = nc.dram_tensor("c_rows", (NSEQ * GPS, NE, GT), F32, kind="Internal").ap()
    with nc.cleanup_on_exit(), ExitStack() as ctx:
        def sb(name, shape, dt=F32):
            return ctx.enter_context(nc.sbuf_tensor(name, shape, dt))

        up_h, dn_h = sb("up_h", [P, NC, KB, P], F32R), sb("dn_h", [P, NC, D], F32R)
        with nc.sbuf_tensor("raw_up", [P, NC, KB, P], F32) as raw_up, nc.sbuf_tensor("raw_dn", [P, NC, D], F32) as raw_dn:
            pass
        up_l, dn_l = sb("up_l", [P, NC, KB, P], F32R), sb("dn_l", [P, NC, D], F32R)
        gw_hl = sb("gw_hl", [P, KB, P], F32R)
        b2_hl = sb("b2_hl", [KC, D], F32R)
        b_up = sb("b_up", [P, NC])
        before = sb("before", [P, NE, NE])
        ctok = sb("ctok", [P, T, 2 * KC])

        raw_gw = sb("raw_gw", [NE, D])
        raw_b2 = sb("raw_b2", [KC, D])
        b2_hi, b2_lo = sb("b2_hi", [KC, D], F32R), sb("b2_lo", [KC, D], F32R)
        lo_row, hi_row = sb("lo_row", [KC, 1]), sb("hi_row", [KC, 1])

        h = [sb(f"hb{u}", [P, T, D]) for u in range(2)]
        xn = sb("xnb", [P, T, D])
        xT_h, xT_l = sb("xTb_h", [P, KB, GT], F32R), sb("xTb_l", [P, KB, GT], F32R)
        act_b = sb("act_b", [P, 2, GT])
        hid_h, hid_l = sb("hid_h", [P, NBUF, GT], F32R), sb("hid_l", [P, NBUF, GT], F32R)
        cT = sb("cT", [KC, GT], F32R)
        cTw = sb("cTw", [NE, GT])
        c_all = sb("c_all", [P, NE, GT])
        c_hi = sb("c_hi", [P, T, NE], F32R)
        glT = sb("glT", [KC, GT])
        s, c8 = sb("s", [P, T, NE]), sb("c8", [P, T, NE])
        gt, eq = sb("gt", [P, T, NE, NE]), sb("eq", [P, T, NE, NE])
        rank = sb("rank", [P, T, NE])
        smax, ssum, csum = sb("smax", [P, T]), sb("ssum", [P, T]), sb("csum", [P, T])
        bn6, mv, var_e = sb("bn6b", [P, T, 6]), sb("mvb", [P, T, 2]), sb("var_eb", [P, T])
        rstd, nmr = sb("rstdb", [P, T]), sb("nmrb", [P, T])

        BY_PE = dict(xT_ps=T, gl_ps=1, lg_ps=1, cT_ps=1, up_ps=NC, down=NC)
        BY_ACT = dict(xT_hi=T, glT=1, s_exp=1, cT_sb=2, relu=NC, hid_hi=NC)
        BY_DVE = dict(ln_bn=T, ln_stats=T, ln_bias=1, xT_lo=T, s_logit=1, s_max=1, s_sub=1, s_sum=1, s_rec=1, s_done=1, gt=1, eq=1,
                      eq_before=1, beaten=1, rank=1, top=1, c_sum=1, c_eps=1, c_rec=1, c_done=1, c_hi=1, c_parts=3, c_lo=1,
                      weighted=NE, hid_lo=NC, h_out=T)
        BY_POOL = dict(ln_var=1, ln_rstd=1, xn_rows=T)
        BY_DMA = {**{f"h_in{t}": 1 for t in range(T)}, **{f"h_stored{t}": 1 for t in range(T)},
                  **{f"c_spread{x}": 1 for x in range(NE)}, "c_out": 1}
        per = {**BY_PE, **BY_ACT, **BY_DVE, **BY_POOL, **BY_DMA}
        sem = {name: nc.alloc_semaphore("B_" + name) for name in per}

        def at(name, g, k=0):
            step = 16 if name in BY_DMA else 1
            return (g + 1) * (per[name] * step) + (k + 1) * step

        def wait(eng, name, g, k=0):
            eng.wait_ge(sem[name], at(name, g, k))

        def new(name):
            return nc.alloc_semaphore("PB_" + name)

        up_in, dn_in = [new(f"up_in{j}") for j in range(NC)], [new(f"dn_in{j}") for j in range(2)]
        gw_in, b2_in, b_in = new("gw_in"), new("b2_in"), new("b_in")
        b2_zero, before_ok, rows_ok = new("b2_zero"), new("before_ok"), new("rows_ok")
        ctok_ones, gw_T, gw_sb = new("ctok_ones"), new("gw_T"), new("gw_sb")
        b2_split, hi, lo, pool_lo = new("b2_split"), new("hi"), new("lo"), new("pool_lo")

        SPLITS = [(up_in[j], raw_up[:, j], up_h[:, j], up_l[:, j]) for j in range(NC)]
        SPLITS += [(dn_in[j >= NS], raw_dn[:, j], dn_h[:, j], dn_l[:, j]) for j in range(NC)]

        POOL_SPLITS = range(NC // 2, 2 * NC, 2)

        def split_lo(eng, n, signal):
            eng.wait_ge(hi, n + 1)
            _, full, hi_t, lo_t = SPLITS[n]
            eng.tensor_tensor(lo_t, full, hi_t.bitcast(F32), ALU.subtract).then_inc(signal, 1)

        def up_load(eng, j):
            w = e["sw1"][:, j * P:(j + 1) * P] if j < NS else e["w1"][j - NS]
            eng.dma_start(raw_up[:, j], blocks(w)).then_inc(up_in[j], 16)

        unread = nc.alloc_semaphore("B_unread")

        def waits_end(eng):
            eng.sem_inc(unread, 1)

        def credit(eng, names, step=1):
            for name in names:
                eng.sem_inc(sem[name], per[name] * step)

        USES = [("gl", "glT", 0), ("up0", "relu", 0), ("lg", "s_logit", 0), ("up1", "relu", 1), ("up2", "relu", 2),
                ("up3", "relu", 3), ("cT", "cT_sb", 1)]
        USES += [(f"up{j}", "relu", j) for j in range(NS, NC)]
        USES += [(f"xT{t}", "xT_lo", t) for t in range(T)]
        RING = 4
        assert NS == RING
        place = {use[0]: i for i, use in enumerate(USES)}

        def ps(use):
            return bank[place[use] % RING]

        def bank_free(pe, use, g):
            i, slot = place[use] - RING, g
            if i < 0:
                slot = g - 1
                i = max(j for j in range(len(USES)) if j % RING == place[use] % RING)
            before_it, signal, k = USES[i]
            wait(pe, signal, slot + 1 if before_it.startswith("xT") else slot, k)

        block = ctx.enter_context(nc.Block())

        def loop(eng, body):
            with eng.Fori(0, NSEQ - 1) as i:
                for u in range(GPS):
                    body(i * GPS + u, u, False)
            for u in range(GPS):
                body((NSEQ - 1) * GPS + u, u, u == GPS - 1)

        @block.sync
        def _(sp):
            credit(sp, BY_DMA, 16)

            def load(g, u):
                for t in range(T):
                    wait(sp, f"h_stored{t}", g - 2)
                    wait(sp, f"h_in{t}", g - 1)
                    sp.dma_start(h[u][:, t, :], h_mid[g, t]).then_inc(sem[f"h_in{t}"], 16)
            sp.dma_start(raw_gw[:, :], e["gate_w"]).then_inc(gw_in, 16)
            for t in range(T):
                sp.dma_start(h[0][:, t, :], h_mid[0, t]).then_inc(sem[f"h_in{t}"], 16)
            for j in range(0, NC, 2):
                up_load(sp, j)
            sp.wait_ge(up_in[1], 16)
            sp.dma_start(raw_dn[:, 0:NS, :], e["sw2"].rearrange("(j p) n -> p j n", p=P)).then_inc(dn_in[0], 16)
            sp.wait_ge(b2_zero, 1)
            for z in range(3):
                sp.dma_start(raw_b2[z * NE:(z + 1) * NE, :], e["b2"]).then_inc(b2_in, 16)
            for z in range(2):
                sp.dma_start(raw_b2[R1 + z:R1 + z + 1, :], e["sb2"].rearrange("(a n) -> a n", a=1)).then_inc(b2_in, 16)

            def body(g, u, last):
                if not last:
                    load(g + 1, (u + 1) % GPS)
                wait(sp, "cT_sb", g, 1)
                sp.dma_start(c_rows[g], cTw[:, :]).then_inc(sem["c_out"], 16)
                wait(sp, "c_out", g)
                for x in range(NE):
                    wait(sp, "weighted", g - 1, x)
                    sp.dma_start(c_all[:, x, :], c_rows[g, x:x + 1].to_broadcast([P, GT])).then_inc(sem[f"c_spread{x}"], 16)
                for t in range(T):
                    wait(sp, "h_out", g, t)
                    sp.dma_start(out_g[g, t], h[u][:, t, :]).then_inc(sem[f"h_stored{t}"], 16)
            loop(sp, body)
            for t in range(T):
                wait(sp, f"h_stored{t}", NSEQ * GPS - 1)

        @block.gpsimd
        def _(pool):
            credit(pool, BY_POOL)
            pool.memset(raw_b2[:, :], 0.0).then_inc(b2_zero, 1)
            pool.memset(before[:], 1.0).then_inc(before_ok, 1)
            pool.memset(lo_row[:], 1.0).then_inc(rows_ok, 1)
            pool.wait_ge(before_ok, 1)
            pool.affine_select(out=before[:], in_=before[:], compare_op=ALU.is_gt, fill=0.0, base=0,
                               pattern=[[1, NE], [-1, NE]], channel_multiplier=0).then_inc(before_ok, 1)
            pool.wait_ge(rows_ok, 1)
            pool.affine_select(out=lo_row[:], in_=lo_row[:], compare_op=ALU.is_ge, fill=0.0, base=-2 * NE,
                               pattern=[[0, 1]], channel_multiplier=1).then_inc(rows_ok, 1)
            pool.wait_ge(rows_ok, 2)
            pool.affine_select(out=lo_row[:], in_=lo_row[:], compare_op=ALU.not_equal, fill=0.0, base=-R1,
                               pattern=[[0, 1]], channel_multiplier=1).then_inc(rows_ok, 1)
            pool.dma_start(b_up[:, 0:NS], e["sb1"].rearrange("(j p) -> p j", p=P), allow_slow_non_contiguous=True)\
                .then_inc(b_in, 16)
            pool.dma_start(b_up[:, NS:NC], e["b1"].rearrange("j p -> p j"), allow_slow_non_contiguous=True)\
                .then_inc(b_in, 16)

            def ln(g, u):
                wait(pool, "ln_stats", g, T - 1)
                wait(pool, "ln_rstd", g - 1)
                waits_end(pool)
                pool.tensor_scalar(var_e[:, :], mv[:, :, 1], LN_EPS, None, ALU.add).then_inc(sem["ln_var"], 1)
                wait(pool, "ln_var", g)
                wait(pool, "xn_rows", g - 1, T - 1)
                pool.tensor_tensor(rstd[:, :], var_e[:, :], half[:, :], ALU.pow).then_inc(sem["ln_rstd"], 1)
                wait(pool, "ln_bias", g)
                for t in range(T):
                    wait(pool, "xT_ps", g - 1, t)
                    waits_end(pool)
                    pool.tensor_scalar(xn[:, t, :], h[u][:, t, :], rstd[:, t:t + 1], nmr[:, t:t + 1],
                                       ALU.mult, ALU.add).then_inc(sem["xn_rows"], 1)
            ln(0, 0)
            for n in POOL_SPLITS:
                split_lo(pool, n, pool_lo)

            def body(g, u, last):
                if not last:
                    ln(g + 1, (u + 1) % GPS)
            loop(pool, body)

        @block.scalar
        def _(act):
            credit(act, BY_ACT)
            for j in range(1, NC, 2):
                up_load(act, j)

            def split_hi(n):
                loaded, full, hi_t, _ = SPLITS[n]
                act.wait_ge(loaded, 16)
                act.activation(hi_t, full, ACT.Copy).then_inc(hi, 1)

            def xT_hi(g):
                for t in range(T):
                    wait(act, "xT_ps", g, t)
                    if t == 0:
                        wait(act, "up_ps", g - 1, NC - 1)
                    act.activation(xT_h[:, :, t * P:(t + 1) * P], ps(f"xT{t}")[:, :].rearrange("p (k n) -> p k n", k=KB),
                                   ACT.Copy).then_inc(sem["xT_hi"], 1)
            for n in range(NC // 2):
                split_hi(n)
                if n == 1:
                    act.dma_start(raw_dn[:, NS:NC, :], e["w2"].rearrange("j p n -> p j n")).then_inc(dn_in[1], 16)
            xT_hi(0)
            for n in range(NC // 2, 2 * NC):
                split_hi(n)
            act.wait_ge(b2_in, 80)
            act.activation(b2_hi[:, :], raw_b2[:, :], ACT.Copy).then_inc(b2_split, 1)
            act.wait_ge(b_in, 32)

            def hid_hi(g, j):
                if j < NS:
                    wait(act, "relu", g, j)
                else:
                    wait(act, "weighted", g, j - NS)
                if j >= NBUF:
                    wait(act, "down", g, j - NBUF)
                else:
                    wait(act, "down", g - 1, NC - NBUF + j)
                act.activation(hid_h[:, j % NBUF, :], act_b[:, j % 2, :], ACT.Copy).then_inc(sem["hid_hi"], 1)

            def body(g, u, last):
                wait(act, "gl_ps", g)
                wait(act, "lg_ps", g - 1)
                act.activation(glT[:, :], ps("gl")[0:KC, :], ACT.Copy).then_inc(sem["glT"], 1)
                for j in range(NC):
                    wait(act, "up_ps", g, j)
                    if j >= 2:
                        wait(act, "hid_lo", g, j - 2)
                    else:
                        wait(act, "hid_lo", g - 1, NC - 2 + j)
                    act.activation(act_b[:, j % 2, :], ps(f"up{j}")[:, :], ACT.Relu, bias=b_up[:, j:j + 1])\
                       .then_inc(sem["relu"], 1)
                    if j == 1:
                        wait(act, "s_sub", g)
                        act.activation(s[:, :, :], s[:, :, :], ACT.Exp).then_inc(sem["s_exp"], 1)
                    if j == NS - 1:
                        wait(act, "cT_ps", g)
                        wait(act, "down", g - 1, NC - 2)
                        act.activation(cT[:, :], ps("cT")[0:KC, :], ACT.Copy).then_inc(sem["cT_sb"], 1)
                        wait(act, "c_out", g - 1)
                        act.activation(cTw[:, :], ps("cT")[KC:KC + NE, :], ACT.Copy).then_inc(sem["cT_sb"], 1)
                    hid_hi(g, j)
                if not last:
                    xT_hi(g + 1)
            loop(act, body)

        @block.tensor
        def _(pe):
            credit(pe, BY_PE)

            def xT(g, slot):
                for t in range(T):
                    wait(pe, "xn_rows", g, t)
                    bank_free(pe, f"xT{t}", slot)
                    for k in range(KB):
                        last = pe.transpose(ps(f"xT{t}")[:, k * P:(k + 1) * P], xn[:, t, k * P:(k + 1) * P],
                                            ident[:, :])
                    last.then_inc(sem["xT_ps"], 1)

            def by_feature(g, use, signal, wh, wl):
                bank_free(pe, use, g)
                for k in range(KB):
                    last = split3(pe, ps(use)[:, :], wh(k), wl(k), xT_h[:, k, :], xT_l[:, k, :], k == 0, k == KB - 1)
                last.then_inc(sem[signal], 1)

            def down(g, j):
                wait(pe, "hid_lo", g, j)
                for t in range(T):
                    if j == 0:
                        wait(pe, "h_out", g - 1, t)
                    cols = slice(t * P, (t + 1) * P)
                    last = split3(pe, bank[RING + t][:, :], hid_h[:, j % NBUF, cols], hid_l[:, j % NBUF, cols],
                                  dn_h[:, j, :], dn_l[:, j, :], j == 0, j == NC - 1)
                last.then_inc(sem["down"], 1)

            pe.wait_ge(gw_in, 16)
            for k in range(KB):
                last = pe.transpose(bank[RING][:, k * NE:(k + 1) * NE], raw_gw[:, k * P:(k + 1) * P], ident[0:NE, 0:NE])
            last.then_inc(gw_T, 1)
            xT(0, -1)
            pe.wait_ge(gw_sb, 3)

            def body(g, u, last_group):
                wait(pe, "xT_lo", g, T - 1)
                bank_free(pe, "gl", g)
                for k in range(KB):
                    pe.matmul(ps("gl")[:, :], gw_hl[:, k, :], xT_h[:, k, :], start=k == 0, stop=False)
                    last = pe.matmul(ps("gl")[:, :], gw_hl[:, k, :], xT_l[:, k, :], start=False, stop=k == KB - 1)
                last.then_inc(sem["gl_ps"], 1)
                for j in range(NC):
                    if u == 0 and j == 0:
                        pe.wait_ge(lo, 1)
                    elif u == 0 and j == 1:
                        pe.wait_ge(lo, 2 * NC - len(POOL_SPLITS))
                        pe.wait_ge(pool_lo, len(POOL_SPLITS))
                        pe.wait_ge(b2_split, 4)
                    by_feature(g, f"up{j}", "up_ps", lambda k: up_h[:, j, k, :], lambda k: up_l[:, j, k, :])
                    if j == 0:
                        wait(pe, "glT", g)
                        bank_free(pe, "lg", g)
                        waits_end(pe)
                        for t in range(T):
                            last = pe.transpose(ps("lg")[:, t * KC:(t + 1) * KC], glT[:, t * P:(t + 1) * P],
                                                ident[0:KC, 0:KC])
                        last.then_inc(sem["lg_ps"], 1)
                    if j >= 2:
                        down(g, j - 2)
                    if j == NC - 1 and not last_group:
                        xT(g + 1, g)
                    if j == NS - 1:
                        wait(pe, "c_lo", g)
                        bank_free(pe, "cT", g)
                        waits_end(pe)
                        for t in range(T):
                            last = pe.transpose(ps("cT")[0:2 * KC, t * P:(t + 1) * P], ctok[:, t, :], ident[:, :])
                        last.then_inc(sem["cT_ps"], 1)
                    if j == NC - 1:
                        wait(pe, "cT_sb", g)
                        for t in range(T):
                            cols = slice(t * P, (t + 1) * P)
                            pe.matmul(bank[RING + t][:, :], cT[:, cols], b2_hl[:, :], start=False, stop=False)
                down(g, NC - 2)
                down(g, NC - 1)
            loop(pe, body)

        @block.vector
        def _(dve):
            credit(dve, BY_DVE)

            def done(ins, name):
                ins.then_inc(sem[name], 1)

            def ln_stats(g, u):
                for t in range(T):
                    wait(dve, f"h_in{t}", g)
                    if t == 0:
                        wait(dve, "ln_var", g - 1)
                        wait(dve, "ln_bias", g - 1)
                    done(dve.bn_stats(bn6[:, t, :], h[u][:, t, :]), "ln_bn")
                for t in range(T):
                    wait(dve, "ln_bn", g, t)
                    waits_end(dve)
                    done(dve.bn_aggr(mv[:, t, :], bn6[:, t, :]), "ln_stats")

            def ln_bias(g):
                wait(dve, "ln_rstd", g)
                wait(dve, "xn_rows", g - 1, T - 1)
                done(dve.scalar_tensor_tensor(nmr[:, :], mv[:, :, 0], -1.0, rstd[:, :], ALU.mult, ALU.mult), "ln_bias")

            def xT_lo(g):
                for t in range(T):
                    wait(dve, "xT_hi", g, t)
                    cols = slice(t * P, (t + 1) * P)
                    done(dve.tensor_tensor(xT_l[:, :, cols], ps(f"xT{t}")[:, :].rearrange("p (k n) -> p k n", k=KB),
                                           xT_h[:, :, cols].bitcast(F32), ALU.subtract), "xT_lo")

            def hid_lo(g, j):
                wait(dve, "hid_hi", g, j)
                done(dve.tensor_tensor(hid_l[:, j % NBUF, :], act_b[:, j % 2, :], hid_h[:, j % NBUF, :].bitcast(F32),
                                       ALU.subtract), "hid_lo")

            def over_experts(a):
                return a[:, :].unsqueeze(2).to_broadcast([P, T, NE])

            def route(g):
                wait(dve, "lg_ps", g)
                lg = ps("lg")[:, 0:T * KC].rearrange("p (t n) -> p t n", t=T)
                done(dve.tensor_reduce(s[:, :, :], lg[:, :, 0:2 * NE].rearrange("p t (z e) -> p t e z", z=2), AX.X,
                                       ALU.add), "s_logit")
                wait(dve, "s_logit", g)
                done(dve.tensor_reduce(smax[:, :], s[:, :, :], AX.X, ALU.max), "s_max")
                wait(dve, "s_max", g)
                done(dve.tensor_tensor(s[:, :, :], s[:, :, :], over_experts(smax), ALU.subtract), "s_sub")

            def top2(g):
                wait(dve, "s_exp", g)
                done(dve.tensor_reduce(ssum[:, :], s[:, :, :], AX.X, ALU.add), "s_sum")
                wait(dve, "s_sum", g)
                done(dve.reciprocal(ssum[:, :], ssum[:, :]), "s_rec")
                wait(dve, "s_rec", g)
                done(dve.tensor_tensor(s[:, :, :], s[:, :, :], over_experts(ssum), ALU.mult), "s_done")
                wait(dve, "s_done", g)
                other = s[:, :, :].unsqueeze(2).to_broadcast([P, T, NE, NE])
                own = s[:, :, :].unsqueeze(3).to_broadcast([P, T, NE, NE])
                done(dve.tensor_tensor(gt[:, :, :, :], other, own, ALU.is_gt), "gt")
                done(dve.tensor_tensor(eq[:, :, :, :], other, own, ALU.is_equal), "eq")
                wait(dve, "eq", g)
                done(dve.tensor_tensor(eq[:, :, :, :], eq[:, :, :, :],
                                       before[:, :, :].unsqueeze(1).to_broadcast([P, T, NE, NE]), ALU.mult), "eq_before")
                wait(dve, "gt", g)
                wait(dve, "eq_before", g)
                done(dve.tensor_tensor(gt[:, :, :, :], gt[:, :, :, :], eq[:, :, :, :], ALU.add), "beaten")
                wait(dve, "beaten", g)
                done(dve.tensor_reduce(rank[:, :, :], gt[:, :, :, :], AX.X, ALU.add), "rank")
                wait(dve, "rank", g)
                done(dve.scalar_tensor_tensor(c8[:, :, :], rank[:, :, :], 1.5, s[:, :, :], ALU.is_lt, ALU.mult), "top")
                wait(dve, "top", g)
                done(dve.tensor_reduce(csum[:, :], c8[:, :, :], AX.X, ALU.add), "c_sum")
                wait(dve, "c_sum", g)
                done(dve.tensor_scalar(csum[:, :], csum[:, :], TOPK_EPS, None, ALU.add), "c_eps")
                wait(dve, "c_eps", g)
                done(dve.reciprocal(csum[:, :], csum[:, :]), "c_rec")
                wait(dve, "c_rec", g)
                done(dve.tensor_tensor(c8[:, :, :], c8[:, :, :], over_experts(csum), ALU.mult), "c_done")
                wait(dve, "c_done", g)
                done(dve.tensor_copy(c_hi[:, :, :], c8[:, :, :]), "c_hi")
                wait(dve, "cT_ps", g - 1)
                done(dve.tensor_copy(ctok[:, :, KC:KC + NE], c8[:, :, :]), "c_parts")
                wait(dve, "c_hi", g)
                for z in (0, 2):
                    done(dve.tensor_copy(ctok[:, :, z * NE:(z + 1) * NE], c_hi[:, :, :].bitcast(F32)), "c_parts")
                done(dve.tensor_tensor(ctok[:, :, NE:2 * NE], c8[:, :, :], c_hi[:, :, :].bitcast(F32), ALU.subtract), "c_lo")

            dve.memset(ctok[:], 0.0).then_inc(ctok_ones, 1)
            dve.memset(gw_hl[:].bitcast(F32), 0.0).then_inc(gw_sb, 1)
            dve.wait_ge(ctok_ones, 1)
            dve.memset(ctok[:, :, R1:R1 + 2], 1.0).then_inc(ctok_ones, 1)
            dve.wait_ge(gw_T, 1)
            dve.wait_ge(gw_sb, 1)
            gate_T = bank[RING][:, 0:KB * NE].rearrange("p (k n) -> p k n", k=KB)
            dve.tensor_copy(gw_hl[:, :, 0:NE], gate_T).then_inc(gw_sb, 1)
            dve.wait_ge(gw_sb, 2)
            dve.tensor_tensor(gw_hl[:, :, NE:2 * NE], gate_T, gw_hl[:, :, 0:NE].bitcast(F32), ALU.subtract).then_inc(gw_sb, 1)
            ln_stats(0, 0)
            ln_bias(0)

            for n in range(NC // 2):
                split_lo(dve, n, lo)
            xT_lo(0)
            for n in range(NC // 2, 2 * NC):
                if n not in POOL_SPLITS:
                    split_lo(dve, n, lo)
            dve.wait_ge(rows_ok, 3)
            dve.tensor_scalar(hi_row[:, :], lo_row[:, :], -1.0, 1.0, ALU.mult, ALU.add).then_inc(rows_ok, 1)
            dve.wait_ge(b2_split, 1)
            dve.tensor_tensor(b2_lo[:, :], raw_b2[:, :], b2_hi[:, :].bitcast(F32), ALU.subtract).then_inc(b2_split, 1)
            dve.wait_ge(b2_split, 2)
            dve.wait_ge(rows_ok, 4)
            dve.tensor_scalar(raw_b2[:, :], b2_hi[:, :].bitcast(F32), hi_row[:, 0:1], None, ALU.mult).then_inc(b2_split, 1)
            dve.wait_ge(b2_split, 3)
            dve.scalar_tensor_tensor(b2_hl[:, :], b2_lo[:, :].bitcast(F32), lo_row[:, 0:1], raw_b2[:, :], ALU.mult,
                                     ALU.add).then_inc(b2_split, 1)
            dve.wait_ge(before_ok, 2)
            dve.wait_ge(ctok_ones, 2)

            def body(g, u, last):
                for j in range(NC):
                    if j >= NS:
                        wait(dve, f"c_spread{j - NS}", g)
                        wait(dve, "relu", g, j)
                        done(dve.tensor_tensor(act_b[:, j % 2, :], act_b[:, j % 2, :], c_all[:, j - NS, :], ALU.mult),
                             "weighted")
                    if j == 1:
                        route(g)
                    hid_lo(g, j)
                    if j == 1:
                        top2(g)
                    if j == NS and not last:
                        ln_stats(g + 1, (u + 1) % GPS)
                    if j == NS + 1 and not last:
                        ln_bias(g + 1)
                if not last:
                    xT_lo(g + 1)
                for t in range(T):
                    wait(dve, "down", g, NC - 1)
                    done(dve.tensor_tensor(h[u][:, t, :], bank[RING + t][:, :], h[u][:, t, :], ALU.add), "h_out")
            loop(dve, body)




def kernel(x, L0_tok_embed_matrix, **weights):
    import numpy as np
    import concourse.bacc as bacc
    from concourse import mybir as _mybir
    from concourse.bass_utils import run_bass_kernel_spmd

    x = np.asarray(x)
    batch, length = x.shape
    arrays = {"x": np.ascontiguousarray(x.reshape(batch, length // P, P).transpose(0, 2, 1)),
              "emb": np.ascontiguousarray(L0_tok_embed_matrix)}
    for name, value in weights.items():
        arrays[name.split("_", 2)[2]] = np.ascontiguousarray(value)
    nc = bacc.Bacc("TRN2", target_bir_lowering=False, num_devices=1)
    args = {n: nc.dram_tensor("in_" + n, a.shape, _mybir.dt.from_np(a.dtype), kind="ExternalInput").ap()
            for n, a in arrays.items()}
    width = arrays["emb"].shape[1]
    out = nc.dram_tensor("out", (batch, length, width), _mybir.dt.from_np(np.dtype("float32")), kind="ExternalOutput").ap()
    lm_tower(nc, args.pop("x"), args.pop("emb"), **args, out=out)
    r = run_bass_kernel_spmd(nc, [{"in_" + n: a for n, a in arrays.items()}], core_ids=[0])
    return r.results[0]["out"]
```
